# Optimizing a Trainium2 kernel written in Bass

```python
import numpy as np
import jax
import jax.numpy as jnp

def _softmax(x, axis=-1):
    return jax.nn.softmax(x, axis=axis)

def _gelu(x):
    return jax.nn.gelu(x, approximate=True)

def _silu(x):
    return jax.nn.silu(x)

def _sigmoid(x):
    return jax.nn.sigmoid(x)

def _layernorm(x, axis=-1, eps=1e-05):
    m = jnp.mean(x, axis=axis, keepdims=True)
    v = jnp.var(x, axis=axis, keepdims=True)
    return (x - m) / jnp.sqrt(v + eps)

def _scatter_add(tgt, idx, src, axis=0):
    return tgt.at[idx].add(src)

def _segment_sum(src, seg, n):
    return jax.ops.segment_sum(src, seg, n)
kernel_name = 'mk_sandwich_d2_jaxref_r8_8b0e7a'

def setup_inputs(seed: int=0):
    np.random.seed(seed)
    _w = jnp.asarray

    def _L0_attn_setup():
        import jax, jax.numpy as jnp
        import numpy as np
        B, S, D, H = (4, 512, 128, 16)
        DH = D // H
        key = jax.random.key(seed)
        ks = jax.random.split(key, 6)
        std = 0.02
        return {'hidden_states': jax.random.normal(ks[0], (B, S, D), jnp.float32), 'Wq': jax.random.normal(ks[1], (D, D), jnp.float32) * std, 'bq': jnp.zeros((D,), jnp.float32), 'Wqa': jax.random.normal(ks[2], (D, H), jnp.float32) * std, 'bqa': jnp.zeros((H,), jnp.float32), 'Wk': jax.random.normal(ks[3], (D, D), jnp.float32) * std, 'bk': jnp.zeros((D,), jnp.float32), 'Wka': jax.random.normal(ks[4], (D, H), jnp.float32) * std, 'bka': jnp.zeros((H,), jnp.float32), 'Wt': jax.random.normal(ks[5], (D, D), jnp.float32) * std, 'bt': jnp.zeros((D,), jnp.float32)}
    _L0_attn_in = _L0_attn_setup()

    def _L0_ffn_setup():
        import jax, jax.numpy as jnp
        import numpy as np
        DIM = 128
        DEPTH = 6
        HEADS = 16
        DIM_HEAD = 64
        WINDOW = 32
        INNER = HEADS * DIM_HEAD
        DIM_INNER = int(DIM * 4 * 2 / 3)
        QK_SCALE = 8.0

        def shift_tokens(t):
            a, s = jnp.split(t, 2, -1)
            s = jnp.pad(s, ((0, 0), (1, 0), (0, 0)))[:, :-1]
            return jnp.concatenate([a, s], -1)

        def l2norm(t):
            return t / jnp.maximum(jnp.linalg.norm(t, axis=-1, keepdims=True), 1e-12)

        def rotate_half(x):
            x1, x2 = jnp.split(x, 2, -1)
            return jnp.concatenate([-x2, x1], -1)

        def rotary_tables(n):
            half = jnp.arange(0, DIM_HEAD, 2, dtype=jnp.float32)
            inv_freq = 1.0 / 10000.0 ** (half / DIM_HEAD)
            t = jnp.arange(n, dtype=jnp.float32)
            freqs = t[:, None] * inv_freq[None, :]
            freqs = jnp.concatenate([freqs, freqs], -1)
            base_scale = (half + 0.4 * DIM_HEAD) / (1.4 * DIM_HEAD)
            power = (t - n // 2) / (WINDOW // 2)
            scale = base_scale[None, :] ** power[:, None]
            scale = jnp.concatenate([scale, scale], -1)
            return (freqs, scale)

        def local_attention(q, k, v):
            b, h, n, d = q.shape
            w = WINDOW
            nw = n // w
            bq = q.reshape(b, h, nw, w, d)
            bk = k.reshape(b, h, nw, w, d)
            bv = v.reshape(b, h, nw, w, d)

            def look(t):
                p = jnp.pad(t, ((0, 0), (0, 0), (1, 0), (0, 0), (0, 0)))
                return jnp.concatenate([p[:, :, :nw], p[:, :, 1:]], axis=3)
            bk2, bv2 = (look(bk), look(bv))
            seq = jnp.arange(n).reshape(nw, w)
            seq_p = jnp.pad(seq, ((1, 0), (0, 0)), constant_values=-1)
            jt = jnp.concatenate([seq_p[:nw], seq_p[1:]], axis=1)
            it = seq[:, :, None]
            jb = jt[:, None, :]
            mask = (it < jb) | (it > jb + w) | (jb == -1)
            sim = jnp.einsum('bhwie,bhwje->bhwij', bq, bk2) * QK_SCALE
            sim = jnp.where(mask, -jnp.finfo(sim.dtype).max, sim)
            attn = jax.nn.softmax(sim, -1)
            out = jnp.einsum('bhwij,bhwje->bhwie', attn, bv2)
            return out.reshape(b, h, n, d)

        def attn_layer(x, Wqkv, qs, ksc, Wo):
            b, n, _ = x.shape
            qkv = x @ Wqkv
            q, k, v = jnp.split(qkv, 3, -1)
            sh = lambda t: t.reshape(b, n, HEADS, DIM_HEAD).transpose(0, 2, 1, 3)
            q, k, v = (sh(q), sh(k), sh(v))
            q = l2norm(q) * qs
            k = l2norm(k) * ksc
            freqs, scale = rotary_tables(n)
            cos, sin = (jnp.cos(freqs), jnp.sin(freqs))
            q = q * cos * scale + rotate_half(q) * sin * scale
            inv = 1.0 / scale
            k = k * cos * inv + rotate_half(k) * sin * inv
            out = local_attention(q, k, v)
            out = out.transpose(0, 2, 1, 3).reshape(b, n, INNER)
            return out @ Wo

        def ffn_layer(x, g, bln, W1, b1, W2, b2):
            mu = x.mean(-1, keepdims=True)
            var = ((x - mu) ** 2).mean(-1, keepdims=True)
            xn = (x - mu) / jnp.sqrt(var + 1e-05) * g + bln
            hg = xn @ W1 + b1
            a, gate = jnp.split(hg, 2, -1)
            return a * jax.nn.gelu(gate, approximate=False) @ W2 + b2
        key = jax.random.key(seed)
        ks = jax.random.split(key, 8)
        B, N = (2, 256)
        init = lambda k, shape: jax.random.normal(k, shape, jnp.float32) * 0.02
        return {'x': jax.random.normal(ks[0], (B, N, DIM), jnp.float32), 'Wqkv': init(ks[1], (DEPTH, DIM, 3 * INNER)), 'q_scale': jnp.ones((DEPTH, DIM_HEAD), jnp.float32), 'k_scale': jnp.ones((DEPTH, DIM_HEAD), jnp.float32), 'Wo': init(ks[2], (DEPTH, INNER, DIM)), 'ln_g': jnp.ones((DEPTH, DIM), jnp.float32), 'ln_b': jnp.zeros((DEPTH, DIM), jnp.float32), 'W1': init(ks[3], (DEPTH, DIM, 2 * DIM_INNER)), 'b1': jnp.zeros((DEPTH, 2 * DIM_INNER), jnp.float32), 'W2': init(ks[4], (DEPTH, DIM_INNER, DIM)), 'b2': jnp.zeros((DEPTH, DIM), jnp.float32)}
    _L0_ffn_in = _L0_ffn_setup()

    def _L1_attn_setup():
        import jax, jax.numpy as jnp
        from jax import lax
        import numpy as np
        D_MODEL, D_STATE, EXPAND, D_CONV = (128, 16, 2, 4)
        D_INNER = EXPAND * D_MODEL
        B, L = (4, 256)

        def _ssm(xl, W_delta, b_delta, W_B, W_C, A_log):
            b, l, d_inner = xl.shape
            A = -jax.nn.softplus(A_log)
            delta = jnp.clip(jax.nn.softplus(xl @ W_delta.T + b_delta), 0.0001, 10.0)
            Bm = xl @ W_B.T
            Cm = xl @ W_C.T

            def step(h, inp):
                d_t, x_t, B_t, C_t = inp
                A_bar = jnp.exp(d_t[:, :, None] * A)
                h = A_bar * h + (d_t * x_t)[:, :, None] * B_t[:, None, :]
                y_t = jnp.einsum('bdn,bn->bd', h, C_t)
                return (h, y_t)
            h0 = jnp.zeros((b, d_inner, A_log.shape[0]), xl.dtype)
            xs = (jnp.swapaxes(delta, 0, 1), jnp.swapaxes(xl, 0, 1), jnp.swapaxes(Bm, 0, 1), jnp.swapaxes(Cm, 0, 1))
            _, ys = lax.scan(step, h0, xs)
            return jnp.swapaxes(ys, 0, 1)
        key = jax.random.key(seed)
        ks = jax.random.split(key, 12)

        def xavier(k, shape):
            fan_in, fan_out = (shape[1], shape[0])
            lim = float(np.sqrt(6.0 / (fan_in + fan_out)))
            return jax.random.uniform(k, shape, jnp.float32, -lim, lim)
        inp = {}
        inp['x'] = jax.random.normal(ks[0], (B, L, D_MODEL), jnp.float32)
        inp['W_left'] = xavier(ks[1], (D_INNER, D_MODEL))
        inp['conv_w'] = jax.random.normal(ks[2], (D_INNER, 1, D_CONV), jnp.float32) * (1.0 / np.sqrt(D_CONV))
        inp['conv_b'] = jax.random.normal(ks[3], (D_INNER,), jnp.float32) * 0.01
        inp['W_delta'] = jax.random.normal(ks[4], (D_INNER, D_INNER), jnp.float32) * (1.0 / np.sqrt(D_INNER))
        inp['b_delta'] = jnp.zeros((D_INNER,), jnp.float32)
        inp['W_B'] = jax.random.normal(ks[5], (D_STATE, D_INNER), jnp.float32) * (1.0 / np.sqrt(D_INNER))
        inp['W_C'] = jax.random.normal(ks[6], (D_STATE, D_INNER), jnp.float32) * (1.0 / np.sqrt(D_INNER))
        inp['A_log'] = jnp.log(jnp.arange(1, D_STATE + 1, dtype=jnp.float32))
        inp['W_right'] = xavier(ks[7], (D_INNER, D_MODEL))
        inp['ln_g'] = jnp.ones((D_INNER,), jnp.float32)
        inp['ln_b'] = jnp.zeros((D_INNER,), jnp.float32)
        inp['W_out'] = xavier(ks[8], (D_MODEL, D_INNER))
        return inp
    _L1_attn_in = _L1_attn_setup()

    def _L1_ffn_setup():
        import jax, jax.numpy as jnp
        import numpy as np
        NUM_EXPERTS = 8
        EXPERT_CAPACITY = 2.0
        key = jax.random.key(seed)
        k1, k2, k3, k4 = jax.random.split(key, 4)
        B, T, C, H, E = (4, 512, 128, 512, NUM_EXPERTS)
        x = jax.random.normal(k1, (B, T, C), jnp.float32)
        gate_w = jax.random.normal(k2, (C, E), jnp.float32) * 0.02
        w1 = jax.random.normal(k3, (E, C, H), jnp.float32) * 0.02
        w2 = jax.random.normal(k4, (E, H, C), jnp.float32) * 0.02
        return {'x': x, 'gate_w': gate_w, 'w1': w1, 'w2': w2}
    _L1_ffn_in = _L1_ffn_setup()
    _d = {'L0_attn_hidden_states': _L0_attn_in['hidden_states'], 'L0_attn_Wq': _L0_attn_in['Wq'], 'L0_attn_bq': _L0_attn_in['bq'], 'L0_attn_Wqa': _L0_attn_in['Wqa'], 'L0_attn_bqa': _L0_attn_in['bqa'], 'L0_attn_Wk': _L0_attn_in['Wk'], 'L0_attn_bk': _L0_attn_in['bk'], 'L0_attn_Wka': _L0_attn_in['Wka'], 'L0_attn_bka': _L0_attn_in['bka'], 'L0_attn_Wt': _L0_attn_in['Wt'], 'L0_attn_bt': _L0_attn_in['bt'], 'L0_ffn_Wqkv': _L0_ffn_in['Wqkv'], 'L0_ffn_q_scale': _L0_ffn_in['q_scale'], 'L0_ffn_k_scale': _L0_ffn_in['k_scale'], 'L0_ffn_Wo': _L0_ffn_in['Wo'], 'L0_ffn_ln_g': _L0_ffn_in['ln_g'], 'L0_ffn_ln_b': _L0_ffn_in['ln_b'], 'L0_ffn_W1': _L0_ffn_in['W1'], 'L0_ffn_b1': _L0_ffn_in['b1'], 'L0_ffn_W2': _L0_ffn_in['W2'], 'L0_ffn_b2': _L0_ffn_in['b2'], 'L1_attn_W_left': _L1_attn_in['W_left'], 'L1_attn_conv_w': _L1_attn_in['conv_w'], 'L1_attn_conv_b': _L1_attn_in['conv_b'], 'L1_attn_W_delta': _L1_attn_in['W_delta'], 'L1_attn_b_delta': _L1_attn_in['b_delta'], 'L1_attn_W_B': _L1_attn_in['W_B'], 'L1_attn_W_C': _L1_attn_in['W_C'], 'L1_attn_A_log': _L1_attn_in['A_log'], 'L1_attn_W_right': _L1_attn_in['W_right'], 'L1_attn_ln_g': _L1_attn_in['ln_g'], 'L1_attn_ln_b': _L1_attn_in['ln_b'], 'L1_attn_W_out': _L1_attn_in['W_out'], 'L1_ffn_gate_w': _L1_ffn_in['gate_w'], 'L1_ffn_w1': _L1_ffn_in['w1'], 'L1_ffn_w2': _L1_ffn_in['w2']}
    _x0 = _d['L0_attn_hidden_states']
    _d['L0_attn_hidden_states'] = jax.random.normal(jax.random.fold_in(jax.random.key(seed), 1), (8, 256, 128), dtype=_x0.dtype)
    del _x0
    return _d

def reference(L0_attn_hidden_states, L0_attn_Wq, L0_attn_bq, L0_attn_Wqa, L0_attn_bqa, L0_attn_Wk, L0_attn_bk, L0_attn_Wka, L0_attn_bka, L0_attn_Wt, L0_attn_bt, L0_ffn_Wqkv, L0_ffn_q_scale, L0_ffn_k_scale, L0_ffn_Wo, L0_ffn_ln_g, L0_ffn_ln_b, L0_ffn_W1, L0_ffn_b1, L0_ffn_W2, L0_ffn_b2, L1_attn_W_left, L1_attn_conv_w, L1_attn_conv_b, L1_attn_W_delta, L1_attn_b_delta, L1_attn_W_B, L1_attn_W_C, L1_attn_A_log, L1_attn_W_right, L1_attn_ln_g, L1_attn_ln_b, L1_attn_W_out, L1_ffn_gate_w, L1_ffn_w1, L1_ffn_w2):

    def _L0_attn_ref(hidden_states, Wq, bq, Wqa, bqa, Wk, bk, Wka, bka, Wt, bt):
        import jax, jax.numpy as jnp
        import numpy as np
        B, S, D, H = (4, 512, 128, 16)
        DH = D // H
        b, s, dm = hidden_states.shape
        h = bqa.shape[0]
        dh = dm // h
        scale = 1.0 / np.sqrt(dh)
        mixed_q = hidden_states @ Wq + bq
        mixed_k = hidden_states @ Wk + bk
        q_score = (mixed_q @ Wqa + bqa) * scale
        q_w = jax.nn.softmax(q_score, axis=1)
        pooled_q = jnp.einsum('bsh,bshd->bhd', q_w, mixed_q.reshape(b, s, h, dh))
        pooled_q = pooled_q.reshape(b, 1, dm)
        mixed_qk = mixed_k * pooled_q
        k_score = (mixed_qk @ Wka + bka) * scale
        k_w = jax.nn.softmax(k_score, axis=1)
        pooled_k = jnp.einsum('bsh,bshd->bhd', k_w, mixed_qk.reshape(b, s, h, dh))
        wv = pooled_k[:, None, :, :] * mixed_q.reshape(b, s, h, dh)
        wv = wv.reshape(b, s, dm)
        return wv @ Wt + bt + mixed_q

    def _L0_ffn_ref(x, Wqkv, q_scale, k_scale, Wo, ln_g, ln_b, W1, b1, W2, b2):
        import jax, jax.numpy as jnp
        import numpy as np
        DIM = 128
        DEPTH = 6
        HEADS = 16
        DIM_HEAD = 64
        WINDOW = 32
        INNER = HEADS * DIM_HEAD
        DIM_INNER = int(DIM * 4 * 2 / 3)
        QK_SCALE = 8.0

        def shift_tokens(t):
            a, s = jnp.split(t, 2, -1)
            s = jnp.pad(s, ((0, 0), (1, 0), (0, 0)))[:, :-1]
            return jnp.concatenate([a, s], -1)

        def l2norm(t):
            return t / jnp.maximum(jnp.linalg.norm(t, axis=-1, keepdims=True), 1e-12)

        def rotate_half(x):
            x1, x2 = jnp.split(x, 2, -1)
            return jnp.concatenate([-x2, x1], -1)

        def rotary_tables(n):
            half = jnp.arange(0, DIM_HEAD, 2, dtype=jnp.float32)
            inv_freq = 1.0 / 10000.0 ** (half / DIM_HEAD)
            t = jnp.arange(n, dtype=jnp.float32)
            freqs = t[:, None] * inv_freq[None, :]
            freqs = jnp.concatenate([freqs, freqs], -1)
            base_scale = (half + 0.4 * DIM_HEAD) / (1.4 * DIM_HEAD)
            power = (t - n // 2) / (WINDOW // 2)
            scale = base_scale[None, :] ** power[:, None]
            scale = jnp.concatenate([scale, scale], -1)
            return (freqs, scale)

        def local_attention(q, k, v):
            b, h, n, d = q.shape
            w = WINDOW
            nw = n // w
            bq = q.reshape(b, h, nw, w, d)
            bk = k.reshape(b, h, nw, w, d)
            bv = v.reshape(b, h, nw, w, d)

            def look(t):
                p = jnp.pad(t, ((0, 0), (0, 0), (1, 0), (0, 0), (0, 0)))
                return jnp.concatenate([p[:, :, :nw], p[:, :, 1:]], axis=3)
            bk2, bv2 = (look(bk), look(bv))
            seq = jnp.arange(n).reshape(nw, w)
            seq_p = jnp.pad(seq, ((1, 0), (0, 0)), constant_values=-1)
            jt = jnp.concatenate([seq_p[:nw], seq_p[1:]], axis=1)
            it = seq[:, :, None]
            jb = jt[:, None, :]
            mask = (it < jb) | (it > jb + w) | (jb == -1)
            sim = jnp.einsum('bhwie,bhwje->bhwij', bq, bk2) * QK_SCALE
            sim = jnp.where(mask, -jnp.finfo(sim.dtype).max, sim)
            attn = jax.nn.softmax(sim, -1)
            out = jnp.einsum('bhwij,bhwje->bhwie', attn, bv2)
            return out.reshape(b, h, n, d)

        def attn_layer(x, Wqkv, qs, ksc, Wo):
            b, n, _ = x.shape
            qkv = x @ Wqkv
            q, k, v = jnp.split(qkv, 3, -1)
            sh = lambda t: t.reshape(b, n, HEADS, DIM_HEAD).transpose(0, 2, 1, 3)
            q, k, v = (sh(q), sh(k), sh(v))
            q = l2norm(q) * qs
            k = l2norm(k) * ksc
            freqs, scale = rotary_tables(n)
            cos, sin = (jnp.cos(freqs), jnp.sin(freqs))
            q = q * cos * scale + rotate_half(q) * sin * scale
            inv = 1.0 / scale
            k = k * cos * inv + rotate_half(k) * sin * inv
            out = local_attention(q, k, v)
            out = out.transpose(0, 2, 1, 3).reshape(b, n, INNER)
            return out @ Wo

        def ffn_layer(x, g, bln, W1, b1, W2, b2):
            mu = x.mean(-1, keepdims=True)
            var = ((x - mu) ** 2).mean(-1, keepdims=True)
            xn = (x - mu) / jnp.sqrt(var + 1e-05) * g + bln
            hg = xn @ W1 + b1
            a, gate = jnp.split(hg, 2, -1)
            return a * jax.nn.gelu(gate, approximate=False) @ W2 + b2
        for i in range(DEPTH):
            x = attn_layer(shift_tokens(x), Wqkv[i], q_scale[i], k_scale[i], Wo[i]) + x
            x = ffn_layer(shift_tokens(x), ln_g[i], ln_b[i], W1[i], b1[i], W2[i], b2[i]) + x
        return x

    def _L1_attn_ref(x, W_left, conv_w, conv_b, W_delta, b_delta, W_B, W_C, A_log, W_right, ln_g, ln_b, W_out):
        import jax, jax.numpy as jnp
        from jax import lax
        import numpy as np
        D_MODEL, D_STATE, EXPAND, D_CONV = (128, 16, 2, 4)
        D_INNER = EXPAND * D_MODEL
        B, L = (4, 256)

        def _ssm(xl, W_delta, b_delta, W_B, W_C, A_log):
            b, l, d_inner = xl.shape
            A = -jax.nn.softplus(A_log)
            delta = jnp.clip(jax.nn.softplus(xl @ W_delta.T + b_delta), 0.0001, 10.0)
            Bm = xl @ W_B.T
            Cm = xl @ W_C.T

            def step(h, inp):
                d_t, x_t, B_t, C_t = inp
                A_bar = jnp.exp(d_t[:, :, None] * A)
                h = A_bar * h + (d_t * x_t)[:, :, None] * B_t[:, None, :]
                y_t = jnp.einsum('bdn,bn->bd', h, C_t)
                return (h, y_t)
            h0 = jnp.zeros((b, d_inner, A_log.shape[0]), xl.dtype)
            xs = (jnp.swapaxes(delta, 0, 1), jnp.swapaxes(xl, 0, 1), jnp.swapaxes(Bm, 0, 1), jnp.swapaxes(Cm, 0, 1))
            _, ys = lax.scan(step, h0, xs)
            return jnp.swapaxes(ys, 0, 1)
        d_conv = conv_w.shape[-1]
        left = x @ W_left.T
        left_ncw = jnp.swapaxes(left, 1, 2)
        left_ncw = jnp.pad(left_ncw, ((0, 0), (0, 0), (d_conv - 1, 0)))
        left_ncw = lax.conv_general_dilated(left_ncw, conv_w, window_strides=(1,), padding='VALID', feature_group_count=conv_w.shape[0]) + conv_b[None, :, None]
        left = jax.nn.silu(jnp.swapaxes(left_ncw, 1, 2))
        ssm_out = _ssm(left, W_delta, b_delta, W_B, W_C, A_log)
        gate = jax.nn.silu(x @ W_right.T)
        out = ssm_out * gate
        mu = jnp.mean(out, axis=-1, keepdims=True)
        var = jnp.mean(jnp.square(out - mu), axis=-1, keepdims=True)
        out = (out - mu) * lax.rsqrt(var + 1e-05) * ln_g + ln_b
        return out @ W_out.T

    def _L1_ffn_ref(x, gate_w, w1, w2):
        import jax, jax.numpy as jnp
        import numpy as np
        NUM_EXPERTS = 8
        EXPERT_CAPACITY = 2.0
        B, T, C = x.shape
        E = gate_w.shape[1]
        cap = int(EXPERT_CAPACITY * T / E)
        scores = jnp.einsum('BTC,CE->BTE', x, gate_w)
        probs = jax.nn.softmax(scores, axis=-1)
        probs_et = jnp.transpose(probs, (0, 2, 1))
        top_p, top_idx = jax.lax.top_k(probs_et, cap)
        xin = jnp.take_along_axis(x[:, None, :, :], top_idx[..., None], axis=2)
        h = jax.nn.gelu(jnp.einsum('BElC,ECH->BElH', xin, w1), approximate=False)
        y = jnp.einsum('BElH,EHC->BElC', h, w2)
        y = y * top_p[..., None]
        b_idx = jnp.arange(B)[:, None, None]
        out = jnp.zeros((B, T, C), x.dtype).at[b_idx, top_idx].add(y)
        return out
    x = L0_attn_hidden_states
    x = x + _layernorm(_L0_attn_ref(_layernorm(x, axis=-1), L0_attn_Wq, L0_attn_bq, L0_attn_Wqa, L0_attn_bqa, L0_attn_Wk, L0_attn_bk, L0_attn_Wka, L0_attn_bka, L0_attn_Wt, L0_attn_bt), axis=-1)
    x = x + _layernorm(_L0_ffn_ref(_layernorm(x, axis=-1), L0_ffn_Wqkv, L0_ffn_q_scale, L0_ffn_k_scale, L0_ffn_Wo, L0_ffn_ln_g, L0_ffn_ln_b, L0_ffn_W1, L0_ffn_b1, L0_ffn_W2, L0_ffn_b2), axis=-1)
    x = x + _layernorm(_L1_attn_ref(_layernorm(x, axis=-1), L1_attn_W_left, L1_attn_conv_w, L1_attn_conv_b, L1_attn_W_delta, L1_attn_b_delta, L1_attn_W_B, L1_attn_W_C, L1_attn_A_log, L1_attn_W_right, L1_attn_ln_g, L1_attn_ln_b, L1_attn_W_out), axis=-1)
    x = x + _layernorm(_L1_ffn_ref(_layernorm(x, axis=-1), L1_ffn_gate_w, L1_ffn_w1, L1_ffn_w2), axis=-1)
    return x

_drawn_inputs = setup_inputs


def setup_inputs(seed=0):
    import zlib

    import numpy as np

    out = dict(_drawn_inputs(seed))
    spreads = {'L0_attn_bq': (0.0, 0.1),
     'L0_attn_bqa': (0.0, 2.0),
     'L0_attn_bk': (0.0, 0.566),
     'L0_attn_bka': (0.0, 2.0),
     'L0_attn_bt': (0.0, 0.1),
     'L0_ffn_q_scale': (1.0, 0.2),
     'L0_ffn_k_scale': (1.0, 0.6),
     'L0_ffn_ln_g': (1.0, 0.6),
     'L0_ffn_ln_b': (0.0, 0.517),
     'L0_ffn_b1': (0.0, 0.1),
     'L0_ffn_b2': (0.0, 0.1),
     'L1_attn_b_delta': (0.0, 0.1),
     'L1_attn_ln_g': (1.0, 0.2),
     'L1_attn_ln_b': (0.0, 0.1)}
    factors = {'L0_attn_Wqa': 33.538, 'L0_attn_Wk': 8.0, 'L0_attn_Wka': 27.218, 'L0_attn_Wt': 4.06}
    for name, (base, spread) in spreads.items():
        noise = np.random.default_rng([zlib.crc32(name.encode()), seed]).standard_normal(out[name].shape)
        drawn = base * np.exp(spread * noise) if base else spread * noise
        out[name] = jnp.asarray(drawn.astype(out[name].dtype))
    for name, factor in factors.items():
        out[name] = (out[name] * factor).astype(out[name].dtype)
    return out
```

```python
from contextlib import ExitStack

import numpy as np

import concourse.bass as bass
from concourse import mybir

F32 = mybir.dt.float32
ALU = mybir.AluOpType
ACT = mybir.ActivationFunctionType
AX = mybir.AxisListType

B, S, C = 8, 256, 128
T = B * S
CH = 512
NCH = T // CH
H0, DH0 = 16, 8
DEPTH, HEADS, DH, WIN = 6, 16, 64, 32
INNER = HEADS * DH
NP = HEADS // 2
UNIT = 512
NU = T // UNIT
DI = 341
FB = [(0, 128), (128, 128), (256, DI - 256)]
LN_EPS = 1e-5
NEG = -3.0e37
ONE_OVER_C = 1.0 / C
DN, DS = 256, 16
E8, CAP, HID = 8, 64, 512
ACT_SET = "natural_log_exp_and_others"


def view(buf, col, *pattern, p0=0, rows=128):
    a = buf[p0:p0 + rows, 0:1]
    return bass.AP(a.tensor, a.offset + col, [[a.ap[0][0], rows]] + [list(x) for x in pattern])


class Pool:

    def __init__(self, nc):
        self.nc, self.sems, self.mem, self.used = nc, ExitStack(), ExitStack(), []

    def __enter__(self):
        return self

    def __exit__(self, *e):
        self.mem.close()
        with self.nc.Block() as block:
            @block.sync
            def _(sp):
                for s in self.used:
                    sp.sem_clear(s)
        self.sems.close()

    def sb(self, name, cols, rows=128):
        return self.mem.enter_context(self.nc.sbuf_tensor(name, [rows, cols], F32))

    def banks(self, name):
        return [self.mem.enter_context(self.nc.psum_tensor(f"{name}{i}", [128, CH], F32)) for i in range(8)]

    def sem(self, name):
        self.used.append(self.sems.enter_context(self.nc.semaphore(name)))
        return self.used[-1]


class Chain:

    def __init__(self, eng, sem):
        self.eng, self.sem, self.n = eng, sem, 0

    def __call__(self, ins):
        ins.then_inc(self.sem, 1)
        self.n += 1
        self.eng.wait_ge(self.sem, self.n)


class Norm:

    def __init__(self, m, con, tag, scratch=None):
        self.mean, self.cen, self.sq, self.var, self.rs0, self.rs, self.out = con.norm_sems
        self.n = con.norms_before * NCH
        con.norms_before += 1
        self.c, self.q = scratch or (m.sb(f"{tag}_c", T), m.sb(f"{tag}_q", T))

    def tensor(self, pe, ones, banks, src, ready):
        for c in range(NCH):
            ready(c)
            pe.matmul(banks[c][:, :], ones[:, :], src[:, c * CH:(c + 1) * CH],
                      start=True, stop=True).then_inc(self.mean, 1)
        for c in range(NCH):
            pe.wait_ge(self.sq, self.n + c + 1)
            pe.matmul(banks[NCH + c][:, :], ones[:, :], self.q[:, c * CH:(c + 1) * CH],
                      start=True, stop=True).then_inc(self.var, 1)

    def vector_centre(self, dve, banks, src):
        for c in range(NCH):
            s = slice(c * CH, (c + 1) * CH)
            dve.wait_ge(self.mean, self.n + c + 1)
            dve.tensor_tensor(self.c[:, s], src[:, s], banks[c][:, :], ALU.subtract).then_inc(self.cen, 1)

    def scalar(self, act, banks, eps):
        for c in range(NCH):
            s = slice(c * CH, (c + 1) * CH)
            act.wait_ge(self.cen, self.n + c + 1)
            act.activation(self.q[:, s], self.c[:, s], ACT.Square).then_inc(self.sq, 1)
        for c in range(NCH):
            s = slice(c * CH, (c + 1) * CH)
            act.wait_ge(self.var, self.n + c + 1)
            act.activation(self.q[:, s], banks[NCH + c][:, :], ACT.Ln, bias=eps).then_inc(self.rs0, 1)
            act.wait_ge(self.rs0, self.n + c + 1)
            act.activation(self.q[:, s], self.q[:, s], ACT.Exp, scale=-0.5).then_inc(self.rs, 1)

    def vector_scale(self, dve, dst):
        for c in range(NCH):
            s = slice(c * CH, (c + 1) * CH)
            dve.wait_ge(self.cen, self.n + c + 1)
            dve.wait_ge(self.rs, self.n + c + 1)
            dve.tensor_tensor(dst[:, s], self.c[:, s], self.q[:, s], ALU.mult).then_inc(self.out, 1)


def load(eng, sem, pairs):
    for to, of in pairs:
        eng.dma_start(to, of).then_inc(sem, 16)
    return 16 * len(pairs)


def additive_attention(nc, io, x, con):
    scale = 1.0 / float(np.sqrt(DH0))
    with Pool(nc) as m:
        wq, wk, wt = m.sb("a_wq", C), m.sb("a_wk", C), m.sb("a_wt", C)
        wqa, wka = m.sb("a_wqa", H0), m.sb("a_wka", H0)
        bias = m.sb("a_bias", 3)
        sbias = m.sb("a_sbias", 2, rows=H0)
        h, q, k = m.sb("a_h", T), m.sb("a_q", T), m.sb("a_k", T)
        w = m.sb("a_w", T, rows=H0)
        mx, sm, rc = (m.sb(f"a_{n}", B, rows=H0) for n in ("max", "sum", "rcp"))
        prod = m.sb("a_prod", T)
        pool_q, pool_k = m.sb("a_poolq", B), m.sb("a_poolk", B)
        bank = m.banks("a_bank")
        n1, n2 = Norm(m, con, "a_ln1"), Norm(m, con, "a_ln2")
        s_load = m.sem("a_load")
        s_qmm, s_kmm, s_q, s_k = m.sem("a_qmm"), m.sem("a_kmm"), m.sem("a_qready"), m.sem("a_kready")
        s_score, s_soft0, s_exp, s_soft, s_wide = (m.sem(f"a_{n}") for n in ("score", "shifted", "exp", "weights", "wide"))
        s_mqk, s_wv, s_tmm, s_y, s_x = (m.sem(f"a_{n}") for n in ("mqk", "wv", "tmm", "y", "x"))
        s_dve, s_dve_pooled = m.sem("a_dve"), m.sem("a_pooled")
        pairs = [(wq[:, :], io["a_wq"]), (wk[:, :], io["a_wk"]), (wt[:, :], io["a_wt"]), (wqa[:, :], io["a_wqa"]),
                  (wka[:, :], io["a_wka"]), (bias[:, 0:1], io["a_bq"]), (bias[:, 1:2], io["a_bk"]),
                  (bias[:, 2:3], io["a_bt"]), (sbias[:, 0:1], io["a_bqa"]), (sbias[:, 1:2], io["a_bka"])]
        n_load = 16 * len(pairs)
        block = m.mem.enter_context(nc.Block())

        @block.sync
        def _(sp):
            load(sp, s_load, pairs)

        @block.tensor
        def _(pe):
            pe.wait_ge(s_load, n_load)
            n1.tensor(pe, con.ones, bank, x, lambda c: None)
            for c in range(NCH):
                pe.wait_ge(n1.out, n1.n + c + 1)
                pe.matmul(bank[c][:, :], wq[:, :], h[:, c * CH:(c + 1) * CH], start=True, stop=True).then_inc(s_qmm, 1)
                pe.matmul(bank[4 + c][:, :], wk[:, :], h[:, c * CH:(c + 1) * CH], start=True, stop=True).then_inc(s_kmm, 1)
            for turn, (src, wgt, done) in enumerate(((q, wqa, s_q), (k, wka, s_mqk))):
                for c in range(NCH):
                    pe.wait_ge(done, c + 1 if turn == 0 else B)
                    pe.matmul(bank[c][0:H0, :], wgt[:, :], src[:, c * CH:(c + 1) * CH],
                              start=True, stop=True).then_inc(s_score, 1)
                for c in range(NCH):
                    pe.wait_ge(s_soft, turn + 1)
                    if turn == 0:
                        pe.wait_ge(s_k, NCH)
                    pe.matmul(bank[4 + c][:, :], con.head8[:, :], w[:, c * CH:(c + 1) * CH],
                              start=True, stop=True).then_inc(s_wide, 1)
            for c in range(NCH):
                pe.wait_ge(s_wv, 2 * c + 2)
                pe.matmul(bank[c][:, :], wt[:, :], h[:, c * CH:(c + 1) * CH], start=True, stop=True).then_inc(s_tmm, 1)
            pe.wait_ge(s_y, NCH)
            n2.tensor(pe, con.ones, bank, prod, lambda c: None)

        @block.scalar
        def _(act):
            nc.scalar.preload_act_table_set(ACT_SET)
            act.wait_ge(s_load, n_load)
            n1.scalar(act, bank, con.eps)
            for c in range(NCH):
                act.wait_ge(s_qmm, c + 1)
                act.activation(q[:, c * CH:(c + 1) * CH], bank[c][:, :], ACT.Identity, bias=bias[:, 0:1]).then_inc(s_q, 1)
            for c in range(NCH):
                act.wait_ge(s_kmm, c + 1)
                act.activation(k[:, c * CH:(c + 1) * CH], bank[4 + c][:, :], ACT.Identity, bias=bias[:, 1:2]).then_inc(s_k, 1)
            for turn in range(2):
                act.wait_ge(s_soft0, turn + 1)
                act.activation(w[:, :], w[:, :], ACT.Exp).then_inc(s_exp, 1)
            for b in range(B):
                if b == 0:
                    act.wait_ge(s_dve_pooled, 2)
                act.activation(h[:, b * S:(b + 1) * S], q[:, b * S:(b + 1) * S], ACT.Copy,
                               scale=pool_k[:, b:b + 1]).then_inc(s_wv, 1)
            n2.scalar(act, bank, con.eps)

        @block.vector
        def _(dve):
            step = Chain(dve, s_dve)
            dve.wait_ge(s_load, n_load)
            n1.vector_centre(dve, bank, x)
            n1.vector_scale(dve, h)
            w3 = view(w, 0, [S, B], [1, S], rows=H0)
            for turn, (src, pooled) in enumerate(((q, pool_q), (k, pool_k))):
                for c in range(NCH):
                    dve.wait_ge(s_score, turn * NCH + c + 1)
                    step(dve.tensor_scalar(w[:, c * CH:(c + 1) * CH], bank[c][0:H0, :], sbias[:, turn:turn + 1],
                                           scale, ALU.add, ALU.mult))
                step(dve.tensor_reduce(mx[:, :], w3, AX.X, ALU.max))
                dve.tensor_tensor(w3, w3, view(mx, 0, [1, B], [0, S], rows=H0), ALU.subtract).then_inc(s_soft0, 1)
                dve.wait_ge(s_exp, turn + 1)
                step(dve.tensor_reduce(sm[:, :], w3, AX.X, ALU.add))
                step(dve.reciprocal(rc[:, :], sm[:, :]))
                dve.tensor_tensor(w3, w3, view(rc, 0, [1, B], [0, S], rows=H0), ALU.mult).then_inc(s_soft, 1)
                for c in range(NCH):
                    dve.wait_ge(s_wide, turn * NCH + c + 1)
                    if turn == 0:
                        dve.wait_ge(s_q, c + 1)
                    step(dve.tensor_tensor(prod[:, c * CH:(c + 1) * CH], bank[4 + c][:, :],
                                           src[:, c * CH:(c + 1) * CH], ALU.mult))
                red = dve.tensor_reduce(pooled[:, :], view(prod, 0, [S, B], [1, S]), AX.X, ALU.add)
                red.then_inc(s_dve_pooled, 1)
                dve.wait_ge(s_dve_pooled, turn + 1)
                if turn == 0:
                    dve.wait_ge(s_k, NCH)
                    for b in range(B):
                        dve.tensor_scalar(k[:, b * S:(b + 1) * S], k[:, b * S:(b + 1) * S], pool_q[:, b:b + 1],
                                          None, ALU.mult).then_inc(s_mqk, 1)
                    dve.wait_ge(s_mqk, B)
            for c in range(NCH):
                dve.wait_ge(s_tmm, c + 1)
                dve.scalar_tensor_tensor(out=prod[:, c * CH:(c + 1) * CH], in0=bank[c][:, :], scalar=bias[:, 2:3],
                                         in1=q[:, c * CH:(c + 1) * CH], op0=ALU.add, op1=ALU.add).then_inc(s_y, 1)
            dve.wait_ge(s_y, NCH)
            n2.vector_centre(dve, bank, prod)
            n2.vector_scale(dve, h)
            dve.wait_ge(n2.out, n2.n + NCH)
            dve.tensor_tensor(x[:, :], x[:, :], h[:, :], ALU.add).then_inc(s_x, 1)


def need(eng, sem, value):
    if not isinstance(value, int) or value > 0:
        eng.wait_ge(sem, value)


def norm_block(nc, m, tag, con, ps, src, dst, add_to=None, scratch=None, sync=None):
    n = Norm(m, con, tag, scratch)
    banks = [view(ps, k * CH, [1, CH]) for k in range(8)]
    s_add = m.sem(f"{tag}_added")
    with nc.Block() as block:
        if sync is not None:
            block.sync(sync)

        @block.tensor
        def _(pe):
            n.tensor(pe, con.ones, banks, src, lambda c: None)

        @block.scalar
        def _(act):
            nc.scalar.preload_act_table_set(ACT_SET)
            n.scalar(act, banks, con.eps)

        @block.vector
        def _(dve):
            n.vector_centre(dve, banks, src)
            n.vector_scale(dve, dst)
            if add_to is not None:
                dve.wait_ge(n.out, n.n + NCH)
                dve.tensor_tensor(add_to[:, :], add_to[:, :], dst[:, :], ALU.add).then_inc(s_add, 1)


def local_attention(nc, io, x, con):
    NI = DEPTH * NU
    LAST = NI - 1
    with Pool(nc) as m:
        y = m.sb("y_t", T)
        ps = m.mem.enter_context(nc.psum_tensor("f_ps", [128, 8 * CH], F32))
        wq, wk, wv, wo = (m.sb(f"f_{n}", INNER) for n in ("wq", "wk", "wv", "wo"))
        w1, w2 = m.sb("f_w1", 2 * DI), m.sb("f_w2", 3 * C)
        cols = m.sb("f_cols", DEPTH * 13)
        fcol = m.sb("f_fcol", 9)
        base_c, base_s = m.sb("f_basec", 2 * S), m.sb("f_bases", 2 * S)
        tab_c, tab_s = m.sb("f_tabc", 2 * S), m.sb("f_tabs", 2 * S)
        same_head, ident = m.sb("f_same", C), m.sb("f_ident", C)
        mask, halves = m.sb("f_mask", 4 * 64), m.sb("f_halves", 2)
        xs = m.sb("f_xs", UNIT)
        v = m.sb("f_v", 8 * CH)
        raw, sq, shuf, rot, rn = (m.sb(f"f_{n}", 2 * UNIT) for n in ("raw", "sq", "shuf", "rot", "rn"))
        KOFF = UNIT + WIN
        qk = [m.sb(f"f_qk{b}", KOFF + UNIT) for b in range(2)]
        s = [m.sb(f"f_s{b}", UNIT) for b in range(2)]
        mx, sm, rc = m.sb("f_max", 8), m.sb("f_sum", 8), m.sb("f_rcp", 8)
        ptz = m.sb("f_ptz", 8 * 96)
        o = m.sb("f_o", NP * UNIT)
        norm_block(nc, m, "f_ln1", con, ps, x, y, scratch=(o, v))
        xs2, cen, sq2, xn = (m.sb(f"f_{n}", UNIT) for n in ("xs2", "cen", "sq2", "xn"))
        gate, hid = m.sb("f_gate", 3 * UNIT), m.sb("f_hid", 3 * UNIT)
        sem = {n: m.sem("f_" + n) for n in (
            "const wv0 wv1 wqk0 wqk1 wo w1 w2 zero xs v_mm v a_mm raw sq n_mm ln rn shuf turned straight rot qk s_mm masked max "
            "shift exp sum rcp p t_mm ptz pv_mm o wo_mm y1 xs2 mean cen sq2 var ln2 rs2 scaled xn g_mm gelu h_mm hid "
            "w2_mm y2 fcol tab seen ahead").split()}
        Y0, H0_, G0 = NU, 1, 1
        GBANK = (2, 0, 1)

        def iterations(eng, slot):
            for j in range(5, 8):
                slot(-1, j, False, True, False)
            for j in range(8):
                slot(0, j, True, True, False)
            with eng.Fori(1, LAST) as i:
                for j in range(8):
                    slot(i, j, True, True, True)
            for j in range(8):
                slot(LAST, j, True, False, True)
            for j in range(8):
                slot(NI, j, False, False, True)

        bank = lambda k, n=1: view(ps, k * CH, *([[CH, n]] if n > 1 else []), [1, CH])

        consts = [(cols[:, :], io["f_cols"]), (base_c[:, :], io["k_cos"]), (base_s[:, :], io["k_sin"]),
                  (same_head[:, :], io["k_same"]), (ident[:, :], io["k_ident"]), (mask[:, :], io["k_mask"]),
                  (halves[:, :], io["k_halves"])]
        n_const = 16 * len(consts)
        body = ExitStack()
        block = body.enter_context(nc.Block())

        @block.sync
        def _(sp):
            def weights(r, t):
                for k, half in enumerate((slice(0, CH), slice(CH, INNER))):
                    need(sp, sem["a_mm"], t * 8 - (4 if k == 0 else 0))
                    sp.dma_start(wq[:, half], io["f_wq"][r][:, half]).then_inc(sem[f"wqk{k}"], 16)
                    sp.dma_start(wk[:, half], io["f_wk"][r][:, half]).then_inc(sem[f"wqk{k}"], 16)
                    need(sp, sem["v_mm"], t * 8 - (4 if k == 0 else 0))
                    sp.dma_start(wv[:, half], io["f_wv"][r][:, half]).then_inc(sem[f"wv{k}"], 16)
                need(sp, sem["wo_mm"], t)
                sp.dma_start(wo[:, :], io["f_wo"][r]).then_inc(sem["wo"], 16)
                need(sp, sem["h_mm"], t * 3)
                sp.dma_start(w1[:, :], io["f_w1"][r]).then_inc(sem["w1"], 16)
                need(sp, sem["w2_mm"], t)
                sp.dma_start(w2[:, :], io["f_w2"][r]).then_inc(sem["w2"], 16)
            load(sp, sem["const"], consts)
            weights(0, 0)
            with sp.Fori(1, DEPTH) as r:
                weights(r, r * NU)

        @block.tensor
        def _(pe):
            def gather(sm_, value):
                if not isinstance(value, int) or value > 0:
                    pe.wait_ge(sm_, value)
                    pe.sem_inc(sem["seen"], 1)

            def values(i, q):
                need(pe, sem["xs"], i + 1)
                need(pe, sem[f"wv{q // 4}"], (i // NU) * 16 + 16)
                need(pe, sem["v"], i * 8 + q)
                if q == 7:
                    need(pe, sem["ln2"], i)
                if q == 0:
                    need(pe, sem["gelu"], i * 3 - 6 + 1 + G0)
                pe.matmul(bank(2), xs[:, 128 * (q % 4):128 * (q % 4) + 128], wv[:, CH * (q // 4):CH * (q // 4) + CH],
                          start=True, stop=True).then_inc(sem["v_mm"], 1)

            def project(i, j):
                need(pe, sem["xs"], i + 1)
                need(pe, sem[f"wqk{j // 4}"], (i // NU) * 32 + 32)
                if j == 0:
                    need(pe, sem["gelu"], i * 3 - 6 + 3 + G0)
                need(pe, sem["ln"], i * 8 + j)
                pe.matmul(bank(0), wq[:, 128 * j:128 * j + 128], xs[:, :], start=True, stop=True)
                pe.matmul(bank(1), wk[:, 128 * j:128 * j + 128], xs[:, :], start=True, stop=True).then_inc(sem["a_mm"], 1)

            def norms(i, j):
                need(pe, sem["sq"], i * 8 + j + 1)
                pe.matmul(bank(0), same_head[:, :], sq[:, 0:UNIT], start=True, stop=True)
                pe.matmul(bank(1), same_head[:, :], sq[:, UNIT:], start=True, stop=True).then_inc(sem["n_mm"], 1)

            def scores(i, j):
                gather(sem["qk"], i * 8 + j + 1)
                gather(sem["masked"], i * 8 + j)
                t = qk[j % 2]
                for w in range(UNIT // WIN):
                    for h in range(2):
                        keys = (view(t, KOFF + WIN * w, [-WIN, 2], [1, WIN], p0=64 * h, rows=64) if w % 2 == 0
                                else view(t, KOFF + WIN * (w - 1), [1, 2 * WIN], p0=64 * h, rows=64))
                        mm = pe.matmul(view(ps, (4 + h) * CH + (w // 4) * 64, [1, 64], p0=WIN * (w % 4), rows=WIN),
                                       t[64 * h:64 * h + 64, WIN * w:WIN * w + WIN], keys, start=True, stop=True)
                mm.then_inc(sem["s_mm"], 1)

            def turn(i, j):
                need(pe, sem["p"], i * 8 + j + 1)
                need(pe, sem["ptz"], i * 8 + j)
                for t in range(4):
                    mm = pe.transpose(view(ps, 6 * CH + 128 * t, [1, 128]), s[j % 2][:, 128 * t:128 * t + 128], ident[:, :])
                mm.then_inc(sem["t_mm"], 1)

            def mix(i, j):
                gather(sem["ptz"], i * 8 + j + 1)
                gather(sem["o"], i * 8 + j)
                if j % 4 == 0:
                    gather(sem["v"], i * 8 + j + 4)
                for p in range(8):
                    n = 96 if p < 7 else 64
                    for h in range(2):
                        mm = pe.matmul(view(ps, 7 * CH + 64 * p, [1, n], p0=64 * h, rows=64),
                                       v[64 * h:64 * h + 64, p * CH + 64 * j:p * CH + 64 * j + 64],
                                       ptz[64 * h:64 * h + 64, 96 * p:96 * p + n],
                                       start=(p == 0), stop=(p == 7), skip_group_check=True)
                mm.then_inc(sem["pv_mm"], 1)

            def wo_part(i, lo, hi):
                need(pe, sem["o"], i * 8 + hi)
                if lo == 0:
                    need(pe, sem["wo"], (i // NU) * 16 + 16)
                    need(pe, sem["y2"], i + Y0)
                for j in range(lo, hi):
                    mm = pe.matmul(bank(3), wo[:, 128 * j:128 * j + 128], o[:, UNIT * j:UNIT * j + UNIT],
                                   start=(j == 0), stop=(j == NP - 1))
                if hi == NP:
                    mm.then_inc(sem["wo_mm"], 1)

            def mean(i):
                need(pe, sem["xs2"], i + 1)
                pe.matmul(bank(3), con.ones[:, :], xs2[:, :], start=True, stop=True).then_inc(sem["mean"], 1)

            def variance(i, run):
                need(pe, sem["sq2"], i + 1)
                if run:
                    need(pe, sem["v"], i * 8 + 8 + 7)
                pe.matmul(bank(2), con.ones[:, :], sq2[:, :], start=True, stop=True).then_inc(sem["var"], 1)

            def gate_mm(i, f):
                if f == 0:
                    need(pe, sem["xn"], i + 1)
                    need(pe, sem["w1"], (i // NU) * 16 + 16)
                f0, n = FB[f]
                pe.matmul(view(ps, GBANK[f] * CH, [1, CH], rows=n), w1[:, DI + f0:DI + f0 + n], xn[:, :],
                          start=True, stop=True).then_inc(sem["g_mm"], 1)

            def hid_mm(i, f):
                if f:
                    need(pe, sem["hid"], i * 3 + f + H0_)
                f0, n = FB[f]
                pe.matmul(view(ps, 3 * CH, [1, CH], rows=n), w1[:, f0:f0 + n], xn[:, :],
                          start=True, stop=True).then_inc(sem["h_mm"], 1)

            def w2_mm(i):
                need(pe, sem["w2"], (i // NU) * 16 + 16)
                need(pe, sem["hid"], i * 3 + 3 + H0_)
                for f, (f0, n) in enumerate(FB):
                    mm = pe.matmul(bank(3), w2[0:n, f * C:f * C + C], hid[0:n, f * UNIT:f * UNIT + UNIT],
                                   start=(f == 0), stop=(f == 2))
                mm.then_inc(sem["w2_mm"], 1)

            def slot(i, j, run, more, before):
                k = i - 1
                has, u, a = (run, i, j + 2) if j < 6 else (more, i + 1, j - 6)
                had1, u1, b1 = (run, i, j - 1) if j >= 1 else (before, k, 7)
                had2, u2, b2 = (run, i, j - 2) if j >= 2 else (before, k, j + 6)
                if run:
                    scores(i, j)
                if before and j == 2:
                    wo_part(k, 6, 8)
                if before and j == 6:
                    need(pe, sem["ln"], i * 8 + 8 if run else 0)
                    gate_mm(k, 1)
                    gate_mm(k, 2)
                if j == 6 and had2:
                    mix(u2, b2)
                if j == 6 and had1:
                    turn(u1, b1)
                if has:
                    project(u, a)
                    values(u, a)
                if j != 6 and had2:
                    mix(u2, b2)
                if before and j < 2:
                    wo_part(k, 3 * j, 3 * j + 3)
                if before and j == 3:
                    mean(k)
                if before and j == 6:
                    hid_mm(k, 1)
                if before and j == 7:
                    hid_mm(k, 2)
                if j != 6 and had1:
                    turn(u1, b1)
                if before and j == 4:
                    variance(k, run)
                if has:
                    norms(u, a)
                if before and j == 5:
                    if run:
                        need(pe, sem["v"], i * 8 + 8)
                    gate_mm(k, 0)
                    hid_mm(k, 0)
                if before and j == 7:
                    w2_mm(k)

            pe.wait_ge(sem["const"], n_const)
            pe.wait_ge(sem["zero"], 1)
            iterations(pe, slot)

        @block.scalar
        def _(act):
            def value_copy(i, q):
                need(act, sem["v_mm"], i * 8 + q + 1)
                if q % 4 == 0:
                    need(act, sem["pv_mm"], i * 8 - 4 + q)
                for r in range(2):
                    for h in range(2):
                        ins = act.activation(view(v, (2 * (q % 4) + r) * CH + 256 * (q // 4), [64, 4], [1, 64], p0=64 * h, rows=64),
                                             view(ps, 2 * CH + 64 * h, [128, 4], [1, 64], p0=64 * r, rows=64), ACT.Copy)
                ins.then_inc(sem["v"], 1)

            def raw_copy(i, j):
                need(act, sem["a_mm"], i * 8 + j + 1)
                need(act, sem["shuf"], i * 8 + j)
                need(act, sem["straight"], i * 8 + j)
                act.activation(view(raw, 0, [UNIT, 2], [1, UNIT]), bank(0, 2), ACT.Copy).then_inc(sem["raw"], 1)
                need(act, sem["raw"], i * 8 + j + 1)
                need(act, sem["n_mm"], i * 8 + j)
                act.activation(sq[:, :], raw[:, :], ACT.Square).then_inc(sem["sq"], 1)

            def inverse_norm(i, j):
                need(act, sem["n_mm"], i * 8 + j + 1)
                need(act, sem["qk"], i * 8 + j)
                act.activation(view(rn, 0, [UNIT, 2], [1, UNIT]), bank(0, 2), ACT.Ln, scale=float(2.0 ** 20)).then_inc(sem["ln"], 1)
                need(act, sem["ln"], i * 8 + j + 1)
                act.activation(rn[:, :], rn[:, :], ACT.Exp, scale=-0.5, bias=con.lift).then_inc(sem["rn"], 1)

            def spread(i, j):
                need(act, sem["t_mm"], i * 8 + j + 1)
                need(act, sem["pv_mm"], i * 8 + j)
                act.activation(view(ptz, 32, [96, 8], [1, 32]), view(ps, 6 * CH + 32, [64, 8], [1, 32]), ACT.Copy)
                act.activation(view(ptz, 0, [96, 8], [1, 32]), view(ps, 6 * CH, [64, 8], [1, 32]), ACT.Copy,
                               scale=halves[:, 0:1])
                act.activation(view(ptz, 64, [96, 7], [1, 32]), view(ps, 6 * CH + 64, [64, 7], [1, 32]), ACT.Copy,
                               scale=halves[:, 1:2]).then_inc(sem["ptz"], 1)

            def out_copy(i, j):
                need(act, sem["pv_mm"], i * 8 + j + 1)
                if j == 0:
                    need(act, sem["wo_mm"], i)
                act.activation(o[:, UNIT * j:UNIT * j + UNIT], bank(7), ACT.Copy).then_inc(sem["o"], 1)

            def gelu(i, f):
                n = FB[f][1]
                need(act, sem["g_mm"], i * 3 + f + 1)
                act.activation(gate[0:n, f * UNIT:f * UNIT + UNIT], view(ps, GBANK[f] * CH, [1, CH], rows=n),
                               ACT.Gelu, bias=fcol[0:n, 5 + f:6 + f]).then_inc(sem["gelu"], 1)

            def slot(i, j, run, more, before):
                k = i - 1
                has, u, a = (run, i, j + 2) if j < 6 else (more, i + 1, j - 6)
                had1, u1, b1 = (run, i, j - 1) if j >= 1 else (before, k, 7)
                had2, u2, b2 = (run, i, j - 2) if j >= 2 else (before, k, j + 6)
                if j == 0:
                    nc.scalar.preload_act_table_set(ACT_SET)
                if before and j == 5:
                    need(act, sem["scaled"], k + 1)
                    act.activation(xn[:, :], xn[:, :], ACT.Identity, scale=fcol[:, 0:1], bias=fcol[:, 1:2]).then_inc(sem["xn"], 1)
                if before and j == 6:
                    gelu(k, 1)
                    gelu(k, 2)
                    nc.scalar.preload_act_table_set(ACT_SET)
                if has:
                    raw_copy(u, a)
                if before and j == 4:
                    need(act, sem["cen"], k + 1)
                    act.activation(sq2[:, :], cen[:, :], ACT.Square).then_inc(sem["sq2"], 1)
                if run:
                    need(act, sem["shift"], i * 8 + j + 1)
                    act.activation(s[j % 2][:, :], s[j % 2][:, :], ACT.Exp, scale=8.0).then_inc(sem["exp"], 1)
                if has:
                    value_copy(u, a)
                if had2:
                    out_copy(u2, b2)
                if had1:
                    spread(u1, b1)
                if has:
                    inverse_norm(u, a)
                if before and j == 4:
                    need(act, sem["var"], k + 1)
                    act.activation(sq2[:, :], bank(2), ACT.Ln, bias=con.eps).then_inc(sem["ln2"], 1)
                    need(act, sem["ln2"], k + 1)
                    act.activation(sq2[:, :], sq2[:, :], ACT.Exp, scale=-0.5).then_inc(sem["rs2"], 1)
                if before and j == 5:
                    gelu(k, 0)

            act.wait_ge(sem["const"], n_const)
            iterations(act, slot)

        @block.gpsimd
        def _(pool):
            def straight(i, j):
                need(pool, sem["raw"], i * 8 + j + 1)
                need(pool, sem["tab"], i + 1)
                need(pool, sem["qk"], i * 8 + j)
                pool.tensor_tensor(view(rot, 0, [S, 4], [1, S]), view(raw, 0, [S, 4], [1, S]),
                                   view(tab_c, 0, [S, 2], [0, 2], [1, S]), ALU.mult).then_inc(sem["straight"], 1)
                need(pool, sem["straight"], i * 8 + j + 1)
                need(pool, sem["turned"], i * 8 + j + 1)
                pool.tensor_tensor(rot[:, :], rot[:, :], shuf[:, :], ALU.add).then_inc(sem["rot"], 1)

            def slot(i, j, run, more, before):
                has, u, a = (run, i, j + 2) if j < 6 else (more, i + 1, j - 6)
                if has:
                    straight(u, a)

            iterations(pool, slot)

        @block.vector
        def _(dve):
            def shift_in(to, unit, done):
                dve.tensor_scalar(to[0:64, :], y[0:64, bass.ds(unit * UNIT, UNIT)], 1.0, None, ALU.mult)
                for b in range(2):
                    mm = dve.tensor_scalar(to[64:128, b * S + 1:b * S + S], y[64:128, bass.ds(unit * UNIT + b * S, S - 1)],
                                           1.0, None, ALU.mult)
                mm.then_inc(done, 1)

            def tables(i):
                need(dve, sem["straight"], i * 8)
                need(dve, sem["turned"], i * 8)
                for k in range(2):
                    for tab, base, n in ((tab_c, base_c, 0), (tab_s, base_s, 1)):
                        ins = dve.tensor_scalar(tab[:, k * S:k * S + S], base[:, k * S:k * S + S],
                                                cols[:, bass.ds((i // NU) * 13 + (2 * k + n), 1)], None, ALU.mult)
                ins.then_inc(sem["tab"], 1)

            def rotate(i, j):
                need(dve, sem["raw"], i * 8 + j + 1)
                need(dve, sem["rot"], i * 8 + j)
                dve.sem_inc(sem["ahead"], 1)
                dve.stream_shuffle(shuf[:, :], raw[:, :], [(p + 16) % 32 for p in range(32)]).then_inc(sem["shuf"], 1)
                need(dve, sem["shuf"], i * 8 + j + 1)
                need(dve, sem["tab"], i + 1)
                dve.tensor_tensor(view(shuf, 0, [S, 4], [1, S]), view(shuf, 0, [S, 4], [1, S]),
                                  view(tab_s, 0, [S, 2], [0, 2], [1, S]), ALU.mult).then_inc(sem["turned"], 1)

            def normalise(i, j):
                need(dve, sem["rot"], i * 8 + j + 1)
                need(dve, sem["rn"], i * 8 + j + 1)
                dve.scalar_tensor_tensor(out=view(qk[j % 2], 0, [KOFF, 2], [1, UNIT]), in0=view(rn, 0, [UNIT, 2], [1, UNIT]),
                                         scalar=1e12, in1=view(rot, 0, [UNIT, 2], [1, UNIT]),
                                         op0=ALU.min, op1=ALU.mult).then_inc(sem["qk"], 1)

            def soft_a(i, j):
                t = s[j % 2]
                need(dve, sem["s_mm"], i * 8 + j + 1)
                need(dve, sem["t_mm"], i * 8 + j - 1)
                dve.tensor_tensor(view(t, 0, [64, 2], [128, 4], [1, 64]), view(ps, 4 * CH, [CH, 2], [64, 4], [1, 64]),
                                  view(mask, 0, [0, 2], [64, 4], [1, 64]), ALU.add).then_inc(sem["masked"], 1)
                need(dve, sem["masked"], i * 8 + j + 1)
                dve.tensor_reduce(mx[:, :], view(t, 0, [64, 8], [1, 64]), AX.X, ALU.max).then_inc(sem["max"], 1)
                need(dve, sem["max"], i * 8 + j + 1)
                dve.tensor_tensor(view(t, 0, [64, 8], [1, 64]), view(t, 0, [64, 8], [1, 64]), view(mx, 0, [1, 8], [0, 64]),
                                  ALU.subtract).then_inc(sem["shift"], 1)

            def soft_b(i, j):
                t = s[j % 2]
                need(dve, sem["exp"], i * 8 + j + 1)
                dve.tensor_reduce(sm[:, :], view(t, 0, [64, 8], [1, 64]), AX.X, ALU.add).then_inc(sem["sum"], 1)
                need(dve, sem["sum"], i * 8 + j + 1)
                dve.reciprocal(rc[:, :], sm[:, :]).then_inc(sem["rcp"], 1)
                need(dve, sem["rcp"], i * 8 + j + 1)
                dve.tensor_tensor(view(t, 0, [64, 8], [1, 64]), view(t, 0, [64, 8], [1, 64]), view(rc, 0, [1, 8], [0, 64]),
                                  ALU.mult).then_inc(sem["p"], 1)

            def hidden(i, f):
                n = FB[f][1]
                need(dve, sem["h_mm"], i * 3 + f + 1)
                need(dve, sem["gelu"], i * 3 + f + 1 + G0)
                dve.scalar_tensor_tensor(out=hid[0:n, f * UNIT:f * UNIT + UNIT], in0=view(ps, 3 * CH, [1, CH], rows=n),
                                         scalar=fcol[0:n, 2 + f:3 + f], in1=gate[0:n, f * UNIT:f * UNIT + UNIT],
                                         op0=ALU.add, op1=ALU.mult).then_inc(sem["hid"], 1)

            def slot(i, j, run, more, before):
                k = i - 1
                has, u, a = (run, i, j + 2) if j < 6 else (more, i + 1, j - 6)
                next1, u1, a1 = (run, i, j + 1) if j < 7 else (more, i + 1, 0)
                ycol = y[:, bass.ds((k % NU) * UNIT, UNIT)] if before else None
                if run:
                    soft_a(i, j)
                if before and j == 6:
                    hidden(k, 0)
                if before and j == 7:
                    hidden(k, 2)
                if next1:
                    normalise(u1, a1)
                if j == 6 and more:
                    tables(i + 1)
                if has:
                    rotate(u, a)
                if before and j == 6:
                    hidden(k, 1)
                if run:
                    soft_b(i, j)
                if before and j == 2:
                    need(dve, sem["wo_mm"], k + 1)
                    dve.tensor_tensor(ycol, ycol, bank(3), ALU.add).then_inc(sem["y1"], 1)
                    need(dve, sem["y1"], k + 1)
                    shift_in(xs2, k % NU, sem["xs2"])
                if before and j == 3:
                    need(dve, sem["gelu"], k * 3 + G0)
                    dve.tensor_scalar(fcol[:, :], cols[:, bass.ds((k // NU) * 13 + 4, 9)], 1.0, None, ALU.mult).then_inc(sem["fcol"], 1)
                    need(dve, sem["mean"], k + 1)
                    need(dve, sem["xs2"], k + 1)
                    dve.tensor_tensor(cen[:, :], xs2[:, :], bank(3), ALU.subtract).then_inc(sem["cen"], 1)
                if before and j == 4:
                    need(dve, sem["rs2"], k + 1)
                    need(dve, sem["fcol"], k + 1)
                    dve.tensor_tensor(xn[:, :], cen[:, :], sq2[:, :], ALU.mult).then_inc(sem["scaled"], 1)
                if before and j == 7:
                    need(dve, sem["w2_mm"], k + 1)
                    dve.scalar_tensor_tensor(out=ycol, in0=bank(3), scalar=fcol[:, 8:9], in1=ycol,
                                             op0=ALU.add, op1=ALU.add).then_inc(sem["y2"], 1)
                if j == 5 and more:
                    need(dve, sem["a_mm"], (i + 1) * 8)
                    need(dve, sem["v_mm"], (i + 1) * 8)
                    need(dve, sem["y2"], i + 2 - NU + Y0)
                    shift_in(xs, (i + 1) % NU, sem["xs"])

            dve.sem_inc(sem["y2"], Y0)
            dve.sem_inc(sem["hid"], H0_)
            dve.sem_inc(sem["gelu"], G0)
            for t in (xs, xs2):
                dve.memset(view(t, 0, [S, 2], [1, 1], p0=64, rows=64), 0.0)
            for t in qk:
                mm = dve.memset(t[:, UNIT:KOFF], 0.0)
            mm.then_inc(sem["zero"], 1)
            dve.wait_ge(sem["zero"], 1)
            dve.wait_ge(sem["const"], n_const)
            iterations(dve, slot)

        body.close()
        norm_block(nc, m, "f_ln2", con, ps, y, o[:, T:2 * T], add_to=x, scratch=(o, v))


def state_space(nc, io, x, con):
    BF16 = mybir.dt.bfloat16
    K = DN // 128
    with Pool(nc) as m:
        ps = m.mem.enter_context(nc.psum_tensor("s_ps", [128, 8 * CH], F32))
        wl, wr = m.sb("s_wl", DN), m.sb("s_wr", DN)
        wd, wbc, wo = m.sb("s_wd", K * DN), m.sb("s_wbc", K * 2 * DS), m.sb("s_wo", K * C)
        cols = m.sb("s_cols", K * 8)
        alog, aneg, ae, al = (m.sb(f"s_{n}", DS) for n in ("alog", "aneg", "ae", "al"))
        ones2 = m.sb("s_ones2", C)
        z = m.sb("s_z", T)
        left, xl, gate, delta, dx = (m.sb(f"s_{n}", K * T) for n in ("left", "xl", "gate", "delta", "dx"))
        bc, res = m.sb("s_bc", T, rows=32), m.sb("s_res", T, rows=32)
        parts = m.mem.enter_context(nc.sbuf_tensor("s_parts", [96, T], BF16))
        bc_part = m.mem.enter_context(nc.sbuf_tensor("s_bcpart", [32, T], BF16))
        pick = m.mem.enter_context(nc.sbuf_tensor("s_pick", [96, 2 * DS * C], BF16))
        decay, st, prod = ([[m.sb(f"s_{n}{par}{k}", T // 2) for k in range(K)] for par in range(2)]
                           for n in ("decay", "state", "prod"))
        bs, cs = ([m.sb(f"s_{n}{par}", T // 2) for par in range(2)] for n in ("bs", "cs"))
        ident = m.sb("s_ident", C)
        ysum, squares = left, xl
        bank = lambda k, n=1, rows=128: view(ps, k * CH, [1, n * CH], rows=rows)

        sem = {n: m.sem("s_" + n) for n in (
            "load pick left_mm left conv xl right_mm gate dpre_mm dpre dabs dexp dlog bc_mm bc split "
            "a_in a0 a1 a2 zero dx fin b_mm c_mm b_in c_in decay drive scan prod acc seen gated mean cen sq var lv rstd nrm aff o_mm o").split()}
        loads = [(wl[:, :], io["s_wl"]), (wr[:, :], io["s_wr"]), (cols[:, :], io["s_cols"]), (wd[:, :], io["s_wd"]),
                 (wbc[:, :], io["s_wbc"]), (wo[:, :], io["s_wo"]), (alog[:, :], io["s_alog"]),
                 (ones2[:, :], io["k_ones2"]), (ident[:, :], io["k_ident"]), (dx[0:96, :], io["k_pick"])]
        n_load = 16 * len(loads)
        norm_block(nc, m, "s_ln1", con, ps, x, z, scratch=(left, xl), sync=lambda sp: load(sp, sem["load"], loads))
        D0, D1 = 2 * K, 2
        body = ExitStack()
        block = body.enter_context(nc.Block())
        part = lambda k, c: slice(k * T + c * CH, k * T + c * CH + CH)
        H = T // 2

        @block.tensor
        def _(pe):
            pe.wait_ge(sem["load"], n_load)
            for c in range(NCH):
                for k in range(K):
                    if c >= 2:
                        pe.wait_ge(sem["left"], 2 * (c - 2) + k + 1)
                    pe.matmul(bank(2 * (c % 2) + k), wl[:, 128 * k:128 * k + 128], z[:, c * CH:c * CH + CH],
                              start=True, stop=True).then_inc(sem["left_mm"], 1)
                for k in range(K):
                    if c:
                        pe.wait_ge(sem["gate"], 2 * (c - 1) + k + 1)
                    pe.matmul(bank(4 + k), wr[:, 128 * k:128 * k + 128], z[:, c * CH:c * CH + CH],
                              start=True, stop=True).then_inc(sem["right_mm"], 1)
            for c in range(NCH):
                pe.wait_ge(sem["xl"], 2 * c + 2)
                for k in range(K):
                    if c >= 2:
                        pe.wait_ge(sem["dpre"], 2 * (c - 2) + k + 1)
                    else:
                        pe.wait_ge(sem["left"], 2 * (c + 2) + k + 1)
                    for r in range(K):
                        mm = pe.matmul(bank(2 * (c % 2) + k), wd[:, r * DN + 128 * k:r * DN + 128 * k + 128],
                                       xl[:, part(r, c)], start=(r == 0), stop=(r == K - 1))
                    mm.then_inc(sem["dpre_mm"], 1)
                if c >= 2:
                    pe.wait_ge(sem["bc"], c - 1)
                for r in range(K):
                    mm = pe.matmul(bank(6 + c % 2, rows=32), wbc[:, 32 * r:32 * r + 32], xl[:, part(r, c)],
                                   start=(r == 0), stop=(r == K - 1))
                mm.then_inc(sem["bc_mm"], 1)
            pe.wait_ge(sem["split"], 6 * NCH)
            pe.wait_ge(sem["pick"], 1)
            pe.wait_ge(sem["dpre"], 2 * NCH)
            pe.wait_ge(sem["bc"], NCH)
            pe.wait_ge(sem["gate"], 2 * NCH)

            def spread(h, n):
                g = h * DS + n
                for half, used, done in ((0, "b_in", "b_mm"), (1, "c_in", "c_mm")):
                    pe.wait_ge(sem[used], g + D1)
                    for c in range(2):
                        mm = pe.matmul(bank(4 + 2 * half + c), pick[:, bass.ds((n + half * DS) * C, C)],
                                       parts[:, h * H + c * CH:h * H + c * CH + CH], start=True, stop=True)
                    mm.then_inc(sem[done], 1)

            def add(h, n, par, first=False):
                g = h * DS + n
                for k in range(K):
                    pe.wait_ge(sem["prod"], g * K + k + 1 + D0)
                    for c in range(2):
                        mm = pe.matmul(bank(2 * k + c), ident[:, :], prod[par][k][:, c * CH:c * CH + CH],
                                       start=first, stop=True, skip_group_check=True)
                    mm.then_inc(sem["acc"], 1)

            for h in range(2):
                for n in range(4):
                    spread(h, n)
                    if n == 2 and h:
                        pe.wait_ge(sem["gated"], K)
                    if n >= 2:
                        add(h, n - 2, n % 2, first=(n == 2))
                with pe.Fori(2, DS // 2) as n2:
                    for par in range(2):
                        spread(h, n2 * 2 + par)
                        add(h, n2 * 2 + (par - 2), par)
                add(h, DS - 2, 0)
                add(h, DS - 1, 1)
            pe.wait_ge(sem["b_in"], 2 * DS + D1 - 1)
            for c in range(NCH):
                pe.wait_ge(sem["gated"], 2 * K)
                for k in range(K):
                    mm = pe.matmul(bank(c), ones2[:, :], ysum[:, part(k, c)], start=(k == 0), stop=(k == K - 1))
                mm.then_inc(sem["mean"], 1)
            for c in range(NCH):
                pe.wait_ge(sem["sq"], K * (c + 1))
                for k in range(K):
                    mm = pe.matmul(bank(4 + c), ones2[:, :], squares[:, part(k, c)], start=(k == 0), stop=(k == K - 1))
                mm.then_inc(sem["var"], 1)
            for c in range(NCH):
                pe.wait_ge(sem["aff"], K * (c + 1))
                for k in range(K):
                    mm = pe.matmul(bank(c), wo[:, C * k:C * k + C], ysum[:, part(k, c)], start=(k == 0), stop=(k == K - 1))
                mm.then_inc(sem["o_mm"], 1)

        @block.scalar
        def _(act):
            def silu_xl(c):
                for k in range(K):
                    act.wait_ge(sem["conv"], 8 * c + 4 * k + 4)
                    act.activation(xl[:, part(k, c)], delta[:, part(k, c)], ACT.Silu).then_inc(sem["xl"], 1)

            def delta_in(c):
                for k in range(K):
                    act.wait_ge(sem["dpre_mm"], 2 * c + k + 1)
                    act.activation(delta[:, part(k, c)], bank(2 * (c % 2) + k), ACT.Identity,
                                   bias=cols[:, 8 * k + 5:8 * k + 6]).then_inc(sem["dpre"], 1)
                act.wait_ge(sem["bc_mm"], c + 1)
                act.activation(bc[:, c * CH:c * CH + CH], bank(6 + c % 2, rows=32), ACT.Copy).then_inc(sem["bc"], 1)
                for k in range(K):
                    act.wait_ge(sem["dpre"], 2 * c + k + 1)
                    act.activation(left[:, part(k, c)], delta[:, part(k, c)], ACT.Abs).then_inc(sem["dabs"], 1)

            act.wait_ge(sem["load"], n_load)
            for c in range(NCH):
                for k in range(K):
                    act.wait_ge(sem["left_mm"], 2 * c + k + 1)
                    act.activation(left[:, part(k, c)], bank(2 * (c % 2) + k), ACT.Copy).then_inc(sem["left"], 1)
                for k in range(K):
                    act.wait_ge(sem["right_mm"], 2 * c + k + 1)
                    act.activation(gate[:, part(k, c)], bank(4 + k), ACT.Silu).then_inc(sem["gate"], 1)
            for c in range(NCH):
                silu_xl(c)
                if c:
                    delta_in(c - 1)
            delta_in(NCH - 1)
            nc.scalar.preload_act_table_set(ACT_SET)
            act.activation(ae[:, :], alog[:, :], ACT.Abs).then_inc(sem["a0"], 1)
            act.wait_ge(sem["a0"], 1)
            act.activation(ae[:, :], ae[:, :], ACT.Exp, scale=-1.0).then_inc(sem["a1"], 1)
            act.wait_ge(sem["a1"], 1)
            act.activation(al[:, :], ae[:, :], ACT.Ln, bias=1.0).then_inc(sem["a2"], 1)

            def soft(h):
                for k in range(K):
                    a = slice(k * T + h * H, k * T + h * H + H)
                    act.wait_ge(sem["dabs"], 4 * h + 4)
                    act.activation(left[:, a], left[:, a], ACT.Exp, scale=-1.0).then_inc(sem["dexp"], 1)
                    act.wait_ge(sem["dexp"], h * K + k + 1)
                    act.activation(left[:, a], left[:, a], ACT.Ln, bias=1.0).then_inc(sem["dlog"], 1)
            soft(0)
            act.wait_ge(sem["a_in"], 3)
            act.wait_ge(sem["zero"], 1)
            nc.scalar.preload_act_table_set(ACT_SET)

            def copy(of, mm, used, to, done, g):
                act.wait_ge(sem[mm], g + 1)
                act.wait_ge(sem[used], g * K - K + D0)
                act.activation(view(to, 0, [1, H]), view(ps, of * CH, [1, H]), ACT.Copy).then_inc(sem[done], 1)

            def step(h, n, par):
                g = h * DS + n
                copy(4, "b_mm", "drive", bs[par], "b_in", g)
                for k in range(K):
                    act.wait_ge(sem["scan"], g * K + k - 2 * K + 1 + D0)
                    act.sem_inc(sem["seen"], 1)
                    act.activation(view(decay[par][k], 1, [S, B // 2], [1, S - 1]),
                                   view(delta, k * T + h * H + 1, [S, B // 2], [1, S - 1]),
                                   ACT.Exp, scale=aneg[:, bass.ds(n, 1)]).then_inc(sem["decay"], 1)
                copy(6, "c_mm", "prod", cs[par], "c_in", g)

            for h in range(2):
                if h:
                    soft(h)
                act.wait_ge(sem["fin"], K * (h + 1))
                with act.Fori(0, DS // 2) as n2:
                    step(h, n2 * 2, 0)
                    step(h, n2 * 2 + 1, 1)
            for c in range(NCH):
                for k in range(K):
                    act.wait_ge(sem["cen"], K * c + k + 1)
                    act.activation(squares[:, part(k, c)], ysum[:, part(k, c)], ACT.Square).then_inc(sem["sq"], 1)
            for c in range(NCH):
                a = slice(c * CH, c * CH + CH)
                act.wait_ge(sem["var"], c + 1)
                act.activation(z[:, a], bank(4 + c), ACT.Ln, bias=con.eps).then_inc(sem["lv"], 1)
                act.wait_ge(sem["lv"], c + 1)
                act.activation(z[:, a], z[:, a], ACT.Exp, scale=-0.5).then_inc(sem["rstd"], 1)
            for c in range(NCH):
                for k in range(K):
                    act.wait_ge(sem["nrm"], K * c + k + 1)
                    act.activation(ysum[:, part(k, c)], ysum[:, part(k, c)], ACT.Identity, scale=cols[:, 8 * k + 6:8 * k + 7],
                                   bias=cols[:, 8 * k + 7:8 * k + 8]).then_inc(sem["aff"], 1)
            for c in range(NCH):
                act.wait_ge(sem["o_mm"], c + 1)
                act.activation(z[:, c * CH:c * CH + CH], bank(c), ACT.Copy).then_inc(sem["o"], 1)

        @block.gpsimd
        def _(pool):
            for par in range(2):
                for k in range(K):
                    zero = pool.memset(view(decay[par][k], 0, [S, B // 2], [1, 1]), 0.0)
            zero.then_inc(sem["zero"], 1)
            pool.wait_ge(sem["load"], n_load)
            pool.tensor_copy(pick[:, :], dx[0:96, :]).then_inc(sem["pick"], 1)

            def step(h, n, par):
                g = h * DS + n
                for k in range(K):
                    pool.wait_ge(sem["scan"], g * K + k + 1 + D0)
                    pool.wait_ge(sem["c_in"], g + 1 + D1)
                    pool.wait_ge(sem["acc"], g * K + k - 2 * K + 1 + D0)
                    pool.tensor_tensor(prod[par][k][:, :], st[par][k][:, :], cs[par][:, :], ALU.mult).then_inc(sem["prod"], 1)

            for h in range(2):
                with pool.Fori(0, DS // 2) as n2:
                    step(h, n2 * 2, 0)
                    step(h, n2 * 2 + 1, 1)

        @block.vector
        def _(dve):
            for n in ("scan", "drive", "prod", "acc"):
                dve.sem_inc(sem[n], D0)
            for n in ("b_in", "c_in"):
                dve.sem_inc(sem[n], D1)
            dve.wait_ge(sem["load"], n_load)
            for c in range(NCH):
                for k in range(K):
                    tap = lambda t: cols[:, 8 * k + t:8 * k + t + 1]
                    at, n = k * T + c * CH, 8 * c + 4 * k
                    dve.wait_ge(sem["left"], 2 * c + k + 1)
                    dve.tensor_scalar(delta[:, part(k, c)], left[:, part(k, c)], tap(3), tap(4), ALU.mult,
                                      ALU.add).then_inc(sem["conv"], 1)
                    for s in range(1, 4):
                        dve.wait_ge(sem["conv"], n + s)
                        dve.scalar_tensor_tensor(out=view(delta, at + s, [S, 2], [1, S - s]),
                                                 in0=view(left, at, [S, 2], [1, S - s]), scalar=tap(3 - s),
                                                 in1=view(delta, at + s, [S, 2], [1, S - s]),
                                                 op0=ALU.mult, op1=ALU.add).then_inc(sem["conv"], 1)
            for c in range(NCH):
                a, n = slice(c * CH, c * CH + CH), 6 * c
                dve.wait_ge(sem["bc"], c + 1)
                dve.tensor_copy(parts[0:32, a], bc[:, a]).then_inc(sem["split"], 1)
                dve.wait_ge(sem["split"], n + 1)
                dve.tensor_tensor(res[:, a], bc[:, a], parts[0:32, a], ALU.subtract).then_inc(sem["split"], 1)
                dve.wait_ge(sem["split"], n + 2)
                dve.tensor_copy(bc_part[:, a], res[:, a]).then_inc(sem["split"], 1)
                dve.wait_ge(sem["split"], n + 3)
                dve.tensor_tensor(bc[:, a], res[:, a], bc_part[:, a], ALU.subtract).then_inc(sem["split"], 1)
                dve.tensor_copy(parts[32:64, a], bc_part[:, a]).then_inc(sem["split"], 1)
                dve.wait_ge(sem["split"], n + 4)
                dve.tensor_copy(parts[64:96, a], bc[:, a]).then_inc(sem["split"], 1)
            dve.wait_ge(sem["a2"], 1)
            dve.tensor_scalar(aneg[:, :], alog[:, :], 0.0, None, ALU.max).then_inc(sem["a_in"], 1)
            dve.wait_ge(sem["a_in"], 1)
            dve.tensor_tensor(aneg[:, :], aneg[:, :], al[:, :], ALU.add).then_inc(sem["a_in"], 1)
            dve.wait_ge(sem["a_in"], 2)
            dve.tensor_scalar(aneg[:, :], aneg[:, :], -1.0, None, ALU.mult).then_inc(sem["a_in"], 1)
            dve.wait_ge(sem["pick"], 1)

            def drives(h):
                for k in range(K):
                    a, n = slice(k * T + h * H, k * T + h * H + H), h * K + k
                    dve.wait_ge(sem["dlog"], n + 1)
                    dve.scalar_tensor_tensor(out=delta[:, a], in0=delta[:, a], scalar=0.0, in1=left[:, a],
                                             op0=ALU.max, op1=ALU.add).then_inc(sem["dx"], 1)
                    dve.wait_ge(sem["dx"], 3 * n + 1)
                    dve.tensor_scalar(delta[:, a], delta[:, a], 1e-4, 10.0, ALU.max, ALU.min).then_inc(sem["dx"], 1)
                    dve.wait_ge(sem["dx"], 3 * n + 2)
                    dve.sem_inc(sem["fin"], 1)
                    dve.tensor_tensor(dx[:, a], delta[:, a], xl[:, a], ALU.mult).then_inc(sem["dx"], 1)
                dve.wait_ge(sem["dx"], 3 * K * (h + 1))
            drives(0)

            def step(h, n, par):
                g = h * DS + n
                for k in range(K):
                    dve.wait_ge(sem["b_in"], g + 1 + D1)
                    dve.wait_ge(sem["prod"], g * K + k - 2 * K + 1 + D0)
                    dve.tensor_tensor(st[par][k][:, :], dx[:, k * T + h * H:k * T + h * H + H], bs[par][:, :],
                                      ALU.mult).then_inc(sem["drive"], 1)
                for k in range(K):
                    dve.wait_ge(sem["drive"], g * K + k + 1 + D0)
                    dve.wait_ge(sem["decay"], g * K + k + 1)
                    dve.tensor_tensor_scan(st[par][k][:, :], decay[par][k][:, :], st[par][k][:, :], 0.0, ALU.mult,
                                           ALU.add).then_inc(sem["scan"], 1)

            for h in range(2):
                with dve.Fori(0, DS // 2) as n2:
                    step(h, n2 * 2, 0)
                    step(h, n2 * 2 + 1, 1)
                if h == 0:
                    drives(1)
                for k in range(K):
                    a = slice(k * T + h * H, k * T + h * H + H)
                    dve.wait_ge(sem["acc"], (h + 1) * DS * K - K + k + 1 + D0)
                    dve.tensor_tensor(ysum[:, a], gate[:, a], view(ps, 2 * k * CH, [1, H]), ALU.mult).then_inc(sem["gated"], 1)
            for c in range(NCH):
                dve.wait_ge(sem["mean"], c + 1)
                for k in range(K):
                    dve.tensor_tensor(ysum[:, part(k, c)], ysum[:, part(k, c)], bank(c), ALU.subtract).then_inc(sem["cen"], 1)
            for c in range(NCH):
                dve.wait_ge(sem["rstd"], c + 1)
                for k in range(K):
                    dve.wait_ge(sem["sq"], K * c + k + 1)
                    dve.tensor_tensor(ysum[:, part(k, c)], ysum[:, part(k, c)], z[:, c * CH:c * CH + CH], ALU.mult).then_inc(sem["nrm"], 1)

        body.close()
        norm_block(nc, m, "s_ln2", con, ps, z, dx[:, 0:T], add_to=x, scratch=(left, xl))


def experts(nc, io, x, con):
    BE, HB = B * E8, HID // 128
    with Pool(nc) as m:
        ps = m.mem.enter_context(nc.psum_tensor("e_ps", [128, 8 * CH], F32))
        gate, ident, iota = m.sb("e_gate", E8), m.sb("e_ident", C), m.sb("e_iota", CAP)
        z, zn = m.sb("e_z", T), m.sb("e_zn", T)
        pn, sn = m.sb("e_pn", 2 * BE), m.sb("e_sn", 2 * BE)
        mx, sm, rc = (m.sb(f"e_{n}", 16) for n in ("max", "sum", "rcp"))
        row, mark, slot = (m.sb(f"e_{n}", S, rows=BE) for n in ("row", "mark", "slot"))
        zero_row = m.sb("e_zero", S, rows=BE)
        top = m.sb("e_top", 8, rows=BE)
        hot, hotp = ([m.sb(f"e_{n}{b}", 2 * 1024) for b in range(2)] for n in ("hot", "hotp"))
        back = m.sb("e_back", 4 * B * S)
        xin = m.sb("e_xin", E8 * CH)
        w1, w2 = ([m.sb(f"e_{n}{b}", HID) for b in range(2)] for n in ("w1", "w2"))
        h = [m.sb(f"e_h{b}", HB * CH) for b in range(2)]
        yout = m.sb("e_y", 4 * 2 * CH)
        bank = lambda k, n=CH, col=0, rows=128: view(ps, k * CH + col, [1, n], rows=rows)
        load_s, w_s = m.sem("e_load"), [m.sem(f"e_weights{b}") for b in range(2)]
        names = ("score max sub exp sum rcp prob zn_mm zn row_mm row top strike mark count slot back_mm sn hot gather xin "
                 "weigh turn_mm back h_mm h y_mm y out_mm out").split()
        sem = {n: m.sem("e_" + n) for n in names}
        loads = [(gate[:, :], io["e_gate"]), (ident[:, :], io["k_ident"]), (iota[:, :], io["k_iota"])]

        def weights(sp, e, b):
            sp.dma_start(w1[b][:, :], io["e_w1"][e]).then_inc(w_s[b], 16)
            sp.dma_start(w2[b][:, :], io["e_w2"][e]).then_inc(w_s[b], 16)

        def first_loads(sp):
            load(sp, load_s, loads)
            for b in range(2):
                weights(sp, b, b)
        norm_block(nc, m, "e_ln1", con, ps, x, z, scratch=(back, xin), sync=first_loads)
        body = ExitStack()
        block = body.enter_context(nc.Block())

        @block.sync
        def _(sp):
            with sp.Fori(1, E8 // 2) as g:
                for b in range(2):
                    sp.wait_ge(sem["y_mm"], 2 * g + b + 1)
                    weights(sp, 2 * g + b, b)

        @block.tensor
        def _(pe):
            pe.wait_ge(load_s, 16 * len(loads))
            for half in range(2):
                for b in range(B):
                    mm = pe.matmul(bank(0, E8, half * BE + b * E8), z[:, (2 * b + half) * 128:(2 * b + half) * 128 + 128],
                                   gate[:, :], start=True, stop=True)
            mm.then_inc(sem["score"], 1)
            for t in range(16):
                mm = pe.transpose(bank(1 + t // 4, 128, 128 * (t % 4)), z[:, 128 * t:128 * t + 128], ident[:, :])
                if t % 4 == 3:
                    mm.then_inc(sem["zn_mm"], 1)
            pe.wait_ge(sem["prob"], 1)
            for half in range(2):
                mm = pe.transpose(bank(5, 128, 128 * half, rows=BE), pn[:, BE * half:BE * half + BE], ident[:, :])
            mm.then_inc(sem["row_mm"], 1)
            pe.wait_ge(sem["slot"], 2)
            for half in range(2):
                mm = pe.transpose(bank(6, BE, BE * half), slot[:, 128 * half:128 * half + 128], ident[0:BE, 0:BE])
            mm.then_inc(sem["back_mm"], 1)

            def gather(g):
                pe.wait_ge(sem["hot"], 2 * g + 2)
                for b in (2 * g, 2 * g + 1):
                    if b == 0:
                        pe.wait_ge(sem["zn"], 4)
                    if b >= 2:
                        pe.wait_ge(sem["xin"], b - 1)
                    for half in range(2):
                        t = 2 * b + half
                        at = half * 1024 + (b % 2) * CH
                        mm = pe.matmul(bank(b % 2), zn[:, 128 * t:128 * t + 128], hot[g % 2][:, at:at + CH],
                                       start=(half == 0), stop=(half == 1))
                    mm.then_inc(sem["gather"], 1)

            def turn(g):
                pe.wait_ge(sem["weigh"], 2 * g + 2)
                for q in range(4):
                    if g:
                        pe.wait_ge(sem["back"], 4 * (g - 1) + q + 1)
                    for p in range(2):
                        for half in range(2):
                            at = half * 1024 + (2 * q + p) * 128
                            mm = pe.transpose(bank(2 + q, 128, p * S + half * 128), hotp[g % 2][:, at:at + 128], ident[:, :])
                    mm.then_inc(sem["turn_mm"], 1)

            gather(0)
            for g in range(4):
                if g < 3:
                    gather(g + 1)
                turn(g)
            pe.wait_ge(sem["back"], 16)
            pe.wait_ge(sem["xin"], B)
            with pe.Fori(0, E8 // 2) as g:
                for b in range(2):
                    pe.wait_ge(w_s[b], (g + 1) * 32)
                    for k in range(HB):
                        pe.wait_ge(sem["h"], (g * 2 + b) * HB + k + 1)
                        pe.matmul(bank(k), w1[b][:, 128 * k:128 * k + 128], xin[:, bass.ds((g * 2 + b) * CH, CH)],
                                  start=True, stop=True).then_inc(sem["h_mm"], 1)
                    pe.wait_ge(sem["h"], (g * 2 + b + 1) * HB + HB)
                    pe.wait_ge(sem["y"], g * 2 + b + 1)
                    for q in range(4):
                        for k in range(HB):
                            mm = pe.matmul(bank(4 + b, 128, 128 * q), h[b][:, k * CH + 128 * q:k * CH + 128 * q + 128],
                                           w2[b][:, 128 * k:128 * k + 128], start=(k == 0), stop=(k == HB - 1))
                    mm.then_inc(sem["y_mm"], 1)
            pe.wait_ge(sem["y"], E8 + 2)
            for b in range(B):
                for p in range(E8 // 2):
                    at = p * 1024 + (b % 2) * CH + (b // 2) * 128
                    mm = pe.matmul(bank(b // 2, S, (b % 2) * S), yout[:, at:at + 128],
                                   back[:, (b * 4 + p) * S:(b * 4 + p) * S + S], start=(p == 0), stop=(p == 3))
                if b % 2:
                    mm.then_inc(sem["out_mm"], 1)

        @block.scalar
        def _(act):
            act.wait_ge(sem["sub"], 1)
            act.activation(pn[:, :], pn[:, :], ACT.Exp).then_inc(sem["exp"], 1)
            for n in range(4):
                act.wait_ge(sem["zn_mm"], n + 1)
                act.activation(zn[:, n * CH:n * CH + CH], bank(1 + n), ACT.Copy).then_inc(sem["zn"], 1)

            def back_copy(g):
                for q in range(4):
                    act.wait_ge(sem["turn_mm"], 4 * g + q + 1)
                    act.activation(back[:, (g * E8 + 2 * q) * S:(g * E8 + 2 * q + 2) * S], bank(2 + q),
                                   ACT.Copy).then_inc(sem["back"], 1)

            for g in range(4):
                for b in (2 * g, 2 * g + 1):
                    act.wait_ge(sem["gather"], b + 1)
                    act.activation(view(xin, b * CAP, [CH, E8], [1, CAP]), view(ps, (b % 2) * CH, [CAP, E8], [1, CAP]),
                                   ACT.Copy).then_inc(sem["xin"], 1)
                if g:
                    back_copy(g - 1)
            back_copy(3)
            with act.Fori(0, E8 // 2) as g:
                for b in range(2):
                    for k in range(HB):
                        act.wait_ge(sem["h_mm"], (g * 2 + b) * HB + k + 1)
                        act.wait_ge(sem["y_mm"], g * 2 + b + 1)
                        act.activation(h[b][:, k * CH:k * CH + CH], bank(k), ACT.Gelu).then_inc(sem["h"], 1)
            for n in range(4):
                act.wait_ge(sem["out_mm"], n + 1)
                act.activation(z[:, n * CH:n * CH + CH], bank(n), ACT.Copy).then_inc(sem["out"], 1)

        @block.gpsimd
        def _(pool):
            for g in range(4):
                for half in range(2):
                    pool.wait_ge(sem["hot"], 2 * g + half + 1)
                    if g >= 2:
                        pool.wait_ge(sem["turn_mm"], 4 * (g - 1))
                    pool.tensor_tensor(view(hotp[g % 2], half * 1024, [CAP, 16], [1, CAP]),
                                       view(hot[g % 2], half * 1024, [CAP, 16], [1, CAP]),
                                       view(pn, half * BE + 2 * g * E8, [1, 16], [0, CAP]), ALU.mult).then_inc(sem["weigh"], 1)

        @block.vector
        def _(dve):
            dve.sem_inc(sem["h"], HB)
            dve.sem_inc(sem["y_mm"], 2)
            dve.sem_inc(sem["y"], 2)
            p3 = view(pn, 0, [E8, 16], [1, E8])
            dve.wait_ge(sem["score"], 1)
            dve.tensor_reduce(mx[:, :], view(ps, 0, [E8, 16], [1, E8]), AX.X, ALU.max).then_inc(sem["max"], 1)
            dve.wait_ge(sem["max"], 1)
            dve.tensor_tensor(p3, view(ps, 0, [E8, 16], [1, E8]), view(mx, 0, [1, 16], [0, E8]), ALU.subtract).then_inc(sem["sub"], 1)
            dve.wait_ge(sem["exp"], 1)
            dve.tensor_reduce(sm[:, :], p3, AX.X, ALU.add).then_inc(sem["sum"], 1)
            dve.wait_ge(sem["sum"], 1)
            dve.reciprocal(rc[:, :], sm[:, :]).then_inc(sem["rcp"], 1)
            dve.wait_ge(sem["rcp"], 1)
            dve.tensor_tensor(p3, p3, view(rc, 0, [1, 16], [0, E8]), ALU.mult).then_inc(sem["prob"], 1)
            dve.wait_ge(sem["row_mm"], 1)
            dve.memset(zero_row[:, :], 0.0)
            dve.tensor_copy(row[:, :], bank(5, S, rows=BE)).then_inc(sem["row"], 1)
            dve.wait_ge(sem["row"], 1)
            for r in range(CAP // 8):
                dve.max(top[:, :], row[:, :]).then_inc(sem["top"], 1)
                dve.wait_ge(sem["top"], r + 1)
                dve.match_replace(row[:, :], top[:, :], row[:, :], -1.0).then_inc(sem["strike"], 1)
                dve.wait_ge(sem["strike"], r + 1)
            dve.tensor_scalar(mark[:, :], row[:, :], 0.0, None, ALU.is_lt).then_inc(sem["mark"], 1)
            dve.wait_ge(sem["mark"], 1)
            dve.tensor_tensor_scan(slot[:, :], mark[:, :], zero_row[:, :], 0.0, ALU.add, ALU.add).then_inc(sem["count"], 1)
            dve.wait_ge(sem["count"], 1)
            dve.tensor_tensor(slot[:, :], slot[:, :], mark[:, :], ALU.mult).then_inc(sem["slot"], 1)
            dve.wait_ge(sem["slot"], 1)
            dve.tensor_scalar(slot[:, :], slot[:, :], -1.0, None, ALU.add).then_inc(sem["slot"], 1)
            dve.wait_ge(sem["back_mm"], 1)
            dve.tensor_copy(sn[:, :], bank(6, 2 * BE)).then_inc(sem["sn"], 1)
            dve.wait_ge(sem["sn"], 1)
            dve.wait_ge(load_s, 16 * len(loads))
            for g in range(4):
                for half in range(2):
                    if g >= 2:
                        dve.wait_ge(sem["gather"], 2 * (g - 1))
                        dve.wait_ge(sem["weigh"], 2 * (g - 1))
                    dve.tensor_tensor(view(hot[g % 2], half * 1024, [CAP, 16], [1, CAP]),
                                      view(sn, half * BE + 2 * g * E8, [1, 16], [0, CAP]),
                                      view(iota, 0, [0, 16], [1, CAP]), ALU.is_equal).then_inc(sem["hot"], 1)
            with dve.Fori(0, E8 // 2) as g:
                for b in range(2):
                    dve.wait_ge(sem["y_mm"], g * 2 + b + 3)
                    for r in range(2):
                        ins = dve.tensor_scalar(yout[64 * b:64 * b + 64, bass.ds(g * 1024 + r * CH, CH)],
                                                view(ps, (4 + b) * CH, [1, CH], p0=64 * r, rows=64), 1.0, None, ALU.mult)
                    ins.then_inc(sem["y"], 1)

        body.close()
        norm_block(nc, m, "e_ln2", con, ps, z, zn, add_to=x, scratch=(back, xin))


class Constants:

    def __init__(self, nc, ctx, io):
        self.norm_sems = [ctx.enter_context(nc.semaphore(f"norm_{x}")) for x in
                          ("mean", "centred", "squared", "var", "logvar", "rstd", "normed")]
        self.norms_before = 0

        def sb(name, cols, rows=128):
            return ctx.enter_context(nc.sbuf_tensor(name, [rows, cols], F32))

        self.ones = sb("k_ones", C)
        self.head8 = sb("k_head8", C, rows=H0)
        self.eps_t = sb("k_eps", 1)
        self.eps = self.eps_t[:, 0:1]
        self.lift_t = sb("k_lift", 1)
        self.lift = self.lift_t[:, 0:1]
        self.loads = [(self.lift_t[:, :], io["k_lift"]), (self.ones[:, :], io["k_ones"]), (self.head8[:, :], io["k_head8"]), (self.eps_t[:, :], io["k_eps"])]


def sandwich(nc, io, out, stages=4, first=1):
    with ExitStack() as sems, ExitStack() as ctx:
        x = ctx.enter_context(nc.sbuf_tensor("x_t", [128, T], F32))
        con = Constants(nc, ctx, io)
        landed = sems.enter_context(nc.semaphore("landed"))
        with nc.Block() as block:
            @block.sync
            def _(sp):
                pairs = [(x[:, c * CH:(c + 1) * CH], io["x"][:, c * CH:(c + 1) * CH]) for c in range(NCH)]
                sp.wait_ge(landed, load(sp, landed, pairs + con.loads))
        if first <= 1:
            additive_attention(nc, io, x, con)
        if first <= 2 <= stages:
            local_attention(nc, io, x, con)
        if first <= 3 <= stages:
            state_space(nc, io, x, con)
        if first <= 4 <= stages:
            experts(nc, io, x, con)
        store = sems.enter_context(nc.semaphore("store"))
        with nc.Block() as block:
            @block.sync
            def _(sp):
                for c in range(NCH):
                    sp.dma_start(out[:, c * CH:(c + 1) * CH], x[:, c * CH:(c + 1) * CH]).then_inc(store, 16)
                sp.wait_ge(store, 16 * NCH)


def dim_order():
    q, r = np.divmod(np.arange(DH), 32)
    order = np.where(r < 16, 16 * q + r, 32 + 16 * q + r - 16)
    return order, (order + 32) % 64


def constants():

    f = np.float32
    k = {"k_ones": np.full((C, C), 1.0 / C, f)}
    k["k_head8"] = np.repeat(np.eye(H0, dtype=f), DH0, axis=1)
    k["k_lift"] = np.full((C, 1), 10 * np.log(2.0), f)
    k["k_ident"] = np.eye(C, dtype=f)
    k["k_same"] = np.kron(np.eye(2, dtype=f), np.ones((DH, DH), f))
    half = np.arange(0, DH, 2, dtype=f)
    freqs = np.arange(S, dtype=f)[:, None] * (f(1.0) / f(10000.0) ** (half / f(DH)))[None, :]
    freqs = np.concatenate([freqs, freqs], -1)
    base = (half + f(0.4 * DH)) / f(1.4 * DH)
    power = (np.arange(S, dtype=f) - f(S // 2)) / f(WIN // 2)
    xscale = base[None, :] ** power[:, None]
    xscale = np.concatenate([xscale, xscale], -1).astype(f)
    order, _ = dim_order()
    sign = np.where(np.arange(DH) < DH // 2, f(-1), f(1))
    for name, t in (("k_cos", np.cos(freqs)), ("k_sin", np.sin(freqs) * sign)):
        qk = np.concatenate([(t * xscale).T[order], (t * (f(1.0) / xscale)).T[order]], 1)
        k[name] = np.ascontiguousarray(np.tile(qk, (2, 1)).astype(f))
    i, c = np.arange(128)[:, None] % WIN, np.arange(2 * WIN)[None, :]
    even = (np.arange(128)[:, None] // WIN) % 2 == 0
    own = (c < WIN) == even
    seen = np.where(own, c % WIN <= i, c % WIN >= i)
    first = seen & (own | (np.arange(128)[:, None] >= WIN))
    k["k_mask"] = np.concatenate([np.where(z, f(0), f(NEG)) for z in (first, seen, first, seen)], 1)
    k["k_ones2"] = np.full((C, C), 1.0 / DN, f)
    pick = np.tile(np.eye(2 * DS, dtype=f)[:, :, None], (3, 1, C)).reshape(6 * DS, 2 * DS * C)
    k["k_pick"] = pick
    k["k_iota"] = np.tile(np.arange(CAP, dtype=f), (C, 1))
    lower = (np.arange(128) % 64 < WIN).astype(f)
    k["k_halves"] = np.stack([lower, 1 - lower], 1)
    k["k_eps"] = np.full((C, 1), LN_EPS, f)
    return k


def arrange(i):
    def col(a):
        return np.ascontiguousarray(np.asarray(a).reshape(-1, 1))

    a = {"x": np.ascontiguousarray(np.asarray(i["L0_attn_hidden_states"]).reshape(T, C).T)}
    for n in ("Wq", "Wk", "Wt", "Wqa", "Wka"):
        a["a_" + n.lower()] = np.ascontiguousarray(i["L0_attn_" + n])
    for n in ("bq", "bk", "bt", "bqa", "bka"):
        a["a_" + n] = col(i["L0_attn_" + n])
    order, partner = dim_order()
    wqkv = np.asarray(i["L0_ffn_Wqkv"]).reshape(DEPTH, C, 3, HEADS, DH)
    a["f_wq"], a["f_wk"] = (np.ascontiguousarray(wqkv[:, :, n][..., order].reshape(DEPTH, C, INNER)) for n in range(2))
    a["f_wv"] = np.ascontiguousarray(wqkv[:, :, 2].reshape(DEPTH, C, INNER))
    a["f_wo"] = np.ascontiguousarray(np.asarray(i["L0_ffn_Wo"]).reshape(DEPTH, NP, 128, C).transpose(0, 2, 1, 3).reshape(DEPTH, 128, INNER))
    a["f_w1"] = np.ascontiguousarray(i["L0_ffn_W1"])
    w2 = np.zeros((DEPTH, 3, 128, C), np.float32)
    b1 = np.zeros((DEPTH, 2, 3, 128), np.float32)
    b1_in = np.asarray(i["L0_ffn_b1"]).reshape(DEPTH, 2, DI)
    for f, (f0, n) in enumerate(FB):
        w2[:, f, :n] = np.asarray(i["L0_ffn_W2"])[:, f0:f0 + n]
        b1[:, :, f, :n] = b1_in[:, :, f0:f0 + n]
    a["f_w2"] = np.ascontiguousarray(w2.transpose(0, 2, 1, 3).reshape(DEPTH, 128, 3 * C))
    cols = np.zeros((128, DEPTH, 13), np.float32)
    for n, name in enumerate(("q_scale", "k_scale")):
        g = np.asarray(i["L0_ffn_" + name]).T
        for t, o in enumerate((order, partner)):
            cols[:, :, 2 * n + t] = np.concatenate([g[o], g[o]], 0)
    cols[:, :, 4], cols[:, :, 5], cols[:, :, 12] = (np.asarray(i["L0_ffn_" + n]).T for n in ("ln_g", "ln_b", "b2"))
    cols[:, :, 6:12] = b1.transpose(3, 0, 1, 2).reshape(128, DEPTH, 6)
    a["f_cols"] = cols.reshape(128, DEPTH * 13)

    def rows(w):
        w = np.asarray(w)
        return np.ascontiguousarray(w.reshape(-1, 128, w.shape[1]).transpose(1, 0, 2).reshape(128, -1))

    L3 = {n[8:]: np.asarray(v) for n, v in i.items() if n.startswith("L1_attn_")}
    a["s_wl"], a["s_wr"] = np.ascontiguousarray(L3["W_left"].T), np.ascontiguousarray(L3["W_right"].T)
    a["s_wd"], a["s_wo"] = rows(L3["W_delta"].T), rows(L3["W_out"].T)
    a["s_wbc"] = rows(np.concatenate([L3["W_B"], L3["W_C"]], 0).T)
    a["s_alog"] = np.ascontiguousarray(np.broadcast_to(L3["A_log"][None, :], (128, DS)))
    a["e_gate"], a["e_w1"] = (np.ascontiguousarray(i["L1_ffn_" + n]) for n in ("gate_w", "w1"))
    a["e_w2"] = np.ascontiguousarray(np.asarray(i["L1_ffn_w2"]).reshape(E8, HID // 128, 128, C).transpose(0, 2, 1, 3).reshape(E8, 128, HID))
    a["s_cols"] = rows(np.concatenate([L3["conv_w"].reshape(DN, 4)] + [L3[n].reshape(DN, 1) for n in
                                      ("conv_b", "b_delta", "ln_g", "ln_b")], 1))
    return a


def kernel(**inputs):
    import concourse.bacc as bacc
    from concourse.bass_utils import run_bass_kernel_spmd

    nc = bacc.Bacc("TRN2", target_bir_lowering=False, num_devices=1)
    arrays = {**arrange(inputs), **constants()}
    io = {n: nc.dram_tensor("in_" + n, a.shape, mybir.dt.from_np(a.dtype), kind="ExternalInput").ap() for n, a in arrays.items()}
    out = nc.dram_tensor("out_x", (C, T), F32, kind="ExternalOutput").ap()
    sandwich(nc, io, out)
    r = run_bass_kernel_spmd(nc, [{"in_" + n: a for n, a in arrays.items()}], core_ids=[0])
    return np.ascontiguousarray(r.results[0]["out_x"].T).reshape(B, S, C)
```

```python
from contextlib import ExitStack

import numpy as np

import concourse.bass as bass
from concourse import mybir

F32 = mybir.dt.float32
ALU = mybir.AluOpType
ACT = mybir.ActivationFunctionType
AX = mybir.AxisListType

B, S, C = 8, 256, 128
T = B * S
CH = 512
NCH = T // CH
H0, DH0 = 16, 8
DEPTH, HEADS, DH, WIN = 6, 16, 64, 32
INNER = HEADS * DH
NP = HEADS // 2
UNIT = 512
NU = T // UNIT
DI = 341
FB = [(0, 128), (128, 128), (256, DI - 256)]
LN_EPS = 1e-5
NEG = -3.0e37
ONE_OVER_C = 1.0 / C
DN, DS = 256, 16
E8, CAP, HID = 8, 64, 512
ACT_SET = "natural_log_exp_and_others"


def view(buf, col, *pattern, p0=0, rows=128):
    a = buf[p0:p0 + rows, 0:1]
    return bass.AP(a.tensor, a.offset + col, [[a.ap[0][0], rows]] + [list(x) for x in pattern])


class Pool:

    def __init__(self, nc):
        self.nc, self.sems, self.mem, self.used = nc, ExitStack(), ExitStack(), []

    def __enter__(self):
        return self

    def __exit__(self, *e):
        self.mem.close()
        with self.nc.Block() as block:
            quarter = (len(self.used) + 3) // 4
            for k, engine in enumerate((block.sync, block.scalar, block.vector, block.gpsimd)):
                @engine
                def _(eng, part=self.used[k * quarter:(k + 1) * quarter]):
                    for s in part:
                        eng.sem_clear(s)
        self.sems.close()

    def sb(self, name, cols, rows=128):
        return self.mem.enter_context(self.nc.sbuf_tensor(name, [rows, cols], F32))

    def banks(self, name):
        return [self.mem.enter_context(self.nc.psum_tensor(f"{name}{i}", [128, CH], F32)) for i in range(8)]

    def sem(self, name):
        self.used.append(self.sems.enter_context(self.nc.semaphore(name)))
        return self.used[-1]


class Norm:

    def __init__(self, m, con, tag, scratch=None):
        self.mean, self.cen, self.sq, self.var, self.rs0, self.rs, self.out = con.norm_sems
        self.n = con.norms_before * NCH
        con.norms_before += 1
        self.c, self.q = scratch or (m.sb(f"{tag}_c", T), m.sb(f"{tag}_q", T))

    def cols(self, c):
        return slice(c * CH, (c + 1) * CH)

    def mean_mm(self, pe, ones, bank, src, c):
        pe.matmul(bank[:, :], ones[:, :], src[:, self.cols(c)], start=True, stop=True).then_inc(self.mean, 1)

    def var_mm(self, pe, ones, bank, c):
        pe.wait_ge(self.sq, self.n + c + 1)
        pe.matmul(bank[:, :], ones[:, :], self.q[:, self.cols(c)], start=True, stop=True).then_inc(self.var, 1)

    def centre(self, dve, bank, src, c):
        dve.wait_ge(self.mean, self.n + c + 1)
        dve.tensor_tensor(self.c[:, self.cols(c)], src[:, self.cols(c)], bank[:, :], ALU.subtract).then_inc(self.cen, 1)

    def square(self, act, c):
        act.wait_ge(self.cen, self.n + c + 1)
        act.activation(self.q[:, self.cols(c)], self.c[:, self.cols(c)], ACT.Square).then_inc(self.sq, 1)

    def root(self, act, bank, eps, c):
        act.wait_ge(self.var, self.n + c + 1)
        act.activation(self.q[:, self.cols(c)], bank[:, :], ACT.Ln, bias=eps).then_inc(self.rs0, 1)
        act.wait_ge(self.rs0, self.n + c + 1)
        act.activation(self.q[:, self.cols(c)], self.q[:, self.cols(c)], ACT.Exp, scale=-0.5).then_inc(self.rs, 1)

    def scale(self, dve, dst, c):
        dve.wait_ge(self.cen, self.n + c + 1)
        dve.wait_ge(self.rs, self.n + c + 1)
        dve.tensor_tensor(dst[:, self.cols(c)], self.c[:, self.cols(c)], self.q[:, self.cols(c)], ALU.mult).then_inc(self.out, 1)

    def add(self, dve, dst, to, added, c):
        dve.wait_ge(self.out, self.n + c + 1)
        dve.tensor_tensor(to[:, self.cols(c)], to[:, self.cols(c)], dst[:, self.cols(c)], ALU.add).then_inc(added, 1)

    def tensor(self, pe, ones, banks, src):
        for c in range(NCH):
            self.mean_mm(pe, ones, banks[c], src, c)
        for c in range(NCH):
            self.var_mm(pe, ones, banks[NCH + c], c)

    def vector_centre(self, dve, banks, src):
        for c in range(NCH):
            self.centre(dve, banks[c], src, c)

    def scalar(self, act, banks, eps):
        for c in range(NCH):
            self.square(act, c)
        for c in range(NCH):
            self.root(act, banks[NCH + c], eps, c)

    def vector_scale(self, dve, dst, add_to=None, added=None):
        for c in range(NCH):
            if add_to is not None and c:
                self.add(dve, dst, add_to, added, c - 1)
            self.scale(dve, dst, c)
        if add_to is not None:
            self.add(dve, dst, add_to, added, NCH - 1)


def load(eng, sem, pairs):
    for to, of in pairs:
        eng.dma_start(to, of).then_inc(sem, 16)
    return 16 * len(pairs)


def additive_attention(nc, io, x, con):
    scale = 1.0 / float(np.sqrt(DH0))
    with Pool(nc) as m:
        wq, wk, wt = m.sb("a_wq", C), m.sb("a_wk", C), m.sb("a_wt", C)
        wqa, wka = m.sb("a_wqa", H0), m.sb("a_wka", H0)
        bias = m.sb("a_bias", 3)
        sbias = m.sb("a_sbias", 2, rows=H0)
        h, q, k = m.sb("a_h", T), m.sb("a_q", T), m.sb("a_k", T)
        w = m.sb("a_w", T, rows=H0)
        mx, low, sm = (m.sb(f"a_{n}", B, rows=H0) for n in ("max", "low", "sum"))
        sb = m.sb("a_sb", 2, rows=H0)
        rc, raw = m.sb("a_rcp", B), m.sb("a_raw", B)
        prod = m.sb("a_prod", T)
        pool_q, pool_k = m.sb("a_poolq", B), m.sb("a_poolk", B)
        bank = m.banks("a_bank")
        n1, n2 = Norm(m, con, "a_ln1"), Norm(m, con, "a_ln2")
        s_load = m.sem("a_load")
        s_qmm, s_kmm, s_q, s_k = m.sem("a_qmm"), m.sem("a_kmm"), m.sem("a_qready"), m.sem("a_kready")
        s_score, s_max, s_low, s_exp, s_wide = (m.sem(f"a_{n}") for n in ("score", "max", "low", "exp", "wide"))
        s_mqk, s_wv, s_tmm, s_y, s_x = (m.sem(f"a_{n}") for n in ("mqk", "wv", "tmm", "y", "x"))
        s_prod, s_pooled = m.sem("a_products"), m.sem("a_pooled")
        pairs = [(wq[:, :], io["a_wq"]), (wk[:, :], io["a_wk"]), (wt[:, :], io["a_wt"]), (wqa[:, :], io["a_wqa"]),
                  (wka[:, :], io["a_wka"]), (bias[:, 0:1], io["a_bq"]), (bias[:, 1:2], io["a_bk"]),
                  (bias[:, 2:3], io["a_bt"]), (sbias[:, 0:1], io["a_bqa"]), (sbias[:, 1:2], io["a_bka"])]
        n_load = 16 * len(pairs)
        block = m.mem.enter_context(nc.Block())

        @block.sync
        def _(sp):
            load(sp, s_load, pairs)

        @block.tensor
        def _(pe):
            n1.tensor(pe, con.ones, bank, x)
            pe.wait_ge(s_load, n_load)
            for c in range(NCH):
                pe.wait_ge(n1.out, n1.n + c + 1)
                pe.matmul(bank[c][:, :], wq[:, :], h[:, c * CH:(c + 1) * CH], start=True, stop=True).then_inc(s_qmm, 1)
                pe.matmul(bank[4 + c][:, :], wk[:, :], h[:, c * CH:(c + 1) * CH], start=True, stop=True).then_inc(s_kmm, 1)
            for turn, (src, wgt, done) in enumerate(((q, wqa, s_q), (k, wka, s_mqk))):
                for c in range(NCH):
                    pe.wait_ge(done, c + 1 if turn == 0 else 2 * c + 2)
                    pe.matmul(bank[c][0:H0, :], wgt[:, :], src[:, c * CH:(c + 1) * CH],
                              start=True, stop=True).then_inc(s_score, 1)
                for c in range(NCH):
                    pe.wait_ge(s_exp, turn * B + 2 * c + 2)
                    if turn == 0:
                        pe.wait_ge(s_k, c + 1)
                    pe.matmul(bank[4 + c][:, :], con.head8[:, :], w[:, c * CH:(c + 1) * CH], start=True, stop=True)
                    pe.matmul(bank[c][:, 0:2], con.head8[:, :], sm[:, 2 * c:2 * c + 2],
                              start=True, stop=True).then_inc(s_wide, 1)
            for c in range(NCH):
                pe.wait_ge(s_wv, 2 * c + 2)
                pe.matmul(bank[c][:, :], wt[:, :], h[:, c * CH:(c + 1) * CH], start=True, stop=True).then_inc(s_tmm, 1)
            pe.wait_ge(s_y, NCH)
            n2.tensor(pe, con.ones, bank, prod)

        @block.scalar
        def _(act):
            nc.scalar.preload_act_table_set(ACT_SET)
            n1.scalar(act, bank, con.eps)
            act.wait_ge(s_load, n_load)
            for c in range(NCH):
                act.wait_ge(s_qmm, c + 1)
                act.activation(q[:, c * CH:(c + 1) * CH], bank[c][:, :], ACT.Identity, bias=bias[:, 0:1]).then_inc(s_q, 1)
            for c in range(NCH):
                act.wait_ge(s_kmm, c + 1)
                act.activation(k[:, c * CH:(c + 1) * CH], bank[4 + c][:, :], ACT.Identity, bias=bias[:, 1:2]).then_inc(s_k, 1)
            for turn in range(2):
                for b in range(B):
                    if b % 2 == 0:
                        act.wait_ge(s_low, turn * NCH + b // 2 + 2)
                    act.activation(w[:, b * S:b * S + S], bank[b // 2][0:H0, (b % 2) * S:(b % 2) * S + S], ACT.Exp,
                                   scale=scale, bias=low[:, b:b + 1], accum_out=sm[:, b:b + 1]).then_inc(s_exp, 1)
            for b in range(B):
                if b % 2 == 0:
                    act.wait_ge(s_pooled, NCH + b // 2 + 1)
                act.activation(h[:, b * S:(b + 1) * S], q[:, b * S:(b + 1) * S], ACT.Copy,
                               scale=pool_k[:, b:b + 1]).then_inc(s_wv, 1)
            n2.scalar(act, bank, con.eps)

        @block.vector
        def _(dve):
            n1.vector_centre(dve, bank, x)
            n1.vector_scale(dve, h)
            dve.wait_ge(s_load, n_load)
            dve.tensor_scalar(sb[:, :], sbias[:, :], scale, None, ALU.mult).then_inc(s_low, 1)
            dve.wait_ge(s_low, 1)
            for turn, (src, pooled) in enumerate(((q, pool_q), (k, pool_k))):
                for c in range(NCH):
                    two, n = slice(2 * c, 2 * c + 2), turn * NCH + c
                    dve.wait_ge(s_score, n + 1)
                    dve.tensor_reduce(mx[:, two], view(bank[c], 0, [S, 2], [1, S], rows=H0), AX.X, ALU.max).then_inc(s_max, 1)
                    dve.wait_ge(s_max, 2 * n + 1)
                    dve.tensor_scalar(mx[:, two], mx[:, two], sbias[:, turn:turn + 1], -scale, ALU.add,
                                      ALU.mult).then_inc(s_max, 1)
                    dve.wait_ge(s_max, 2 * n + 2)
                    dve.tensor_scalar(low[:, two], mx[:, two], sb[:, turn:turn + 1], None, ALU.add).then_inc(s_low, 1)
                for c in range(NCH):
                    a, two, n = slice(c * CH, c * CH + CH), slice(2 * c, 2 * c + 2), turn * NCH + c
                    dve.wait_ge(s_wide, n + 1)
                    dve.reciprocal(rc[:, two], bank[c][:, 0:2]).then_inc(s_prod, 1)
                    if turn == 0:
                        dve.wait_ge(s_q, c + 1)
                    dve.tensor_tensor(prod[:, a], bank[4 + c][:, :], src[:, a], ALU.mult).then_inc(s_prod, 1)
                    dve.wait_ge(s_prod, 3 * n + 2)
                    dve.tensor_reduce(raw[:, two], view(prod, c * CH, [S, 2], [1, S]), AX.X, ALU.add).then_inc(s_prod, 1)
                    dve.wait_ge(s_prod, 3 * n + 3)
                    dve.tensor_tensor(pooled[:, two], raw[:, two], rc[:, two], ALU.mult).then_inc(s_pooled, 1)
                    dve.wait_ge(s_pooled, n + 1)
                    if turn == 0:
                        dve.wait_ge(s_k, c + 1)
                        for b in (2 * c, 2 * c + 1):
                            dve.tensor_scalar(k[:, b * S:(b + 1) * S], k[:, b * S:(b + 1) * S], pool_q[:, b:b + 1],
                                              None, ALU.mult).then_inc(s_mqk, 1)
                dve.wait_ge(s_mqk, B)
            for c in range(NCH):
                dve.wait_ge(s_tmm, c + 1)
                dve.scalar_tensor_tensor(out=prod[:, c * CH:(c + 1) * CH], in0=bank[c][:, :], scalar=bias[:, 2:3],
                                         in1=q[:, c * CH:(c + 1) * CH], op0=ALU.add, op1=ALU.add).then_inc(s_y, 1)
            dve.wait_ge(s_y, NCH)
            n2.vector_centre(dve, bank, prod)
            n2.vector_scale(dve, h, x, s_x)


def need(eng, sem, value):
    if not isinstance(value, int) or value > 0:
        eng.wait_ge(sem, value)


def local_attention(nc, io, x, con):
    NI = DEPTH * NU
    LAST = NI - 1
    with Pool(nc) as m:
        y = m.sb("y_t", T)
        ps = m.mem.enter_context(nc.psum_tensor("f_ps", [128, 8 * CH], F32))
        wq, wk, wv, wo = (m.sb(f"f_{n}", INNER) for n in ("wq", "wk", "wv", "wo"))
        w1, w2 = m.sb("f_w1", 2 * DI), m.sb("f_w2", 3 * C)
        cols = m.sb("f_cols", DEPTH * 13)
        fcol = m.sb("f_fcol", 9)
        base_c, base_s = m.sb("f_basec", 2 * S), m.sb("f_bases", 2 * S)
        tab_c, tab_s = m.sb("f_tabc", 2 * S), m.sb("f_tabs", 2 * S)
        same_head, ident = m.sb("f_same", C), m.sb("f_ident", C)
        mask, halves = m.sb("f_mask", 4 * 64), m.sb("f_halves", 2)
        xs = m.sb("f_xs", UNIT)
        v = m.sb("f_v", 8 * CH)
        raw, sq, shuf, rot, rn = (m.sb(f"f_{n}", 2 * UNIT) for n in ("raw", "sq", "shuf", "rot", "rn"))
        KOFF = UNIT + WIN
        qk = [m.sb(f"f_qk{b}", KOFF + UNIT) for b in range(2)]
        s = [m.sb(f"f_s{b}", UNIT) for b in range(2)]
        mx, sm, rc = m.sb("f_max", 8), m.sb("f_sum", 8), m.sb("f_rcp", 8)
        ptz = m.sb("f_ptz", 8 * 96)
        o = m.sb("f_o", NP * UNIT)
        xs2, cen, sq2, xn = (m.sb(f"f_{n}", UNIT) for n in ("xs2", "cen", "sq2", "xn"))
        gate, hid = m.sb("f_gate", 3 * UNIT), m.sb("f_hid", 3 * UNIT)
        sem = {n: m.sem("f_" + n) for n in (
            "const wv0 wv1 wqk0 wqk1 wo w1 w2 zero xs v_mm v a_mm raw sq n_mm ln rn shuf turned straight rot qk s_mm masked max "
            "shift exp sum rcp p t_mm ptz pv_mm o wo_mm y1 xs2 mean cen sq2 var ln2 rs2 scaled xn g_mm gelu h_mm hid "
            "w2_mm y2 fcol tab seen ahead").split()}
        bank = lambda k, n=1: view(ps, k * CH, *([[CH, n]] if n > 1 else []), [1, CH])
        Y0, H0_, G0 = NU, 1, 1
        GBANK = (2, 0, 1)

        n2_out = o[:, T:2 * T]
        n2_bank = [bank(4 + c) for c in range(NCH)]
        added = m.sem("f_added")
        ended = lambda c: NI - NU + c + 1 + Y0

        def iterations(eng, slot, behind):
            for j in range(5, 8):
                slot(-1, j, False, True, False)
            for j in range(8):
                slot(0, j, True, True, False)
            with eng.Fori(1, LAST) as i:
                for j in range(8):
                    slot(i, j, True, True, True)
            for j in range(8):
                slot(LAST, j, True, False, True)
            for j in range(8):
                slot(NI, j, False, False, True)
                behind(j)


        consts = [(cols[:, :], io["f_cols"]), (base_c[:, :], io["k_cos"]), (base_s[:, :], io["k_sin"]),
                  (same_head[:, :], io["k_same"]), (ident[:, :], io["k_ident"]), (mask[:, :], io["k_mask"]),
                  (halves[:, :], io["k_halves"])]
        n_const = 16 * len(consts)

        def weights(sp, r, t):
            for k, half in enumerate((slice(0, CH), slice(CH, INNER))):
                need(sp, sem["a_mm"], t * 8 - (4 if k == 0 else 0))
                sp.dma_start(wq[:, half], io["f_wq"][r][:, half]).then_inc(sem[f"wqk{k}"], 16)
                sp.dma_start(wk[:, half], io["f_wk"][r][:, half]).then_inc(sem[f"wqk{k}"], 16)
                need(sp, sem["v_mm"], t * 8 - (4 if k == 0 else 0))
                sp.dma_start(wv[:, half], io["f_wv"][r][:, half]).then_inc(sem[f"wv{k}"], 16)
            need(sp, sem["wo_mm"], t)
            sp.dma_start(wo[:, :], io["f_wo"][r]).then_inc(sem["wo"], 16)
            need(sp, sem["h_mm"], t * 3)
            sp.dma_start(w1[:, :], io["f_w1"][r]).then_inc(sem["w1"], 16)
            need(sp, sem["w2_mm"], t)
            sp.dma_start(w2[:, :], io["f_w2"][r]).then_inc(sem["w2"], 16)

        n1 = Norm(m, con, "f_ln1", (o, o[:, T:2 * T]))
        n1_banks = [bank(k) for k in range(8)]
        n2 = Norm(m, con, "f_ln2", (v, v[:, T:2 * T]))
        body = ExitStack()
        block = body.enter_context(nc.Block())

        @block.sync
        def _(sp):
            load(sp, sem["const"], consts)
            weights(sp, 0, 0)
            with sp.Fori(1, DEPTH) as r:
                weights(sp, r, r * NU)

        @block.tensor
        def _(pe):
            def gather(sm_, value):
                if not isinstance(value, int) or value > 0:
                    pe.wait_ge(sm_, value)
                    pe.sem_inc(sem["seen"], 1)

            def values(i, q):
                need(pe, sem["xs"], i + 1)
                need(pe, sem[f"wv{q // 4}"], (i // NU) * 16 + 16)
                need(pe, sem["v"], i * 8 + q)
                if q == 7:
                    need(pe, sem["ln2"], i)
                if q == 0:
                    need(pe, sem["gelu"], i * 3 - 6 + 1 + G0)
                pe.matmul(bank(2), xs[:, 128 * (q % 4):128 * (q % 4) + 128], wv[:, CH * (q // 4):CH * (q // 4) + CH],
                          start=True, stop=True).then_inc(sem["v_mm"], 1)

            def project(i, j):
                need(pe, sem["xs"], i + 1)
                need(pe, sem[f"wqk{j // 4}"], (i // NU) * 32 + 32)
                if j == 0:
                    need(pe, sem["gelu"], i * 3 - 6 + 3 + G0)
                need(pe, sem["ln"], i * 8 + j)
                pe.matmul(bank(0), wq[:, 128 * j:128 * j + 128], xs[:, :], start=True, stop=True)
                pe.matmul(bank(1), wk[:, 128 * j:128 * j + 128], xs[:, :], start=True, stop=True).then_inc(sem["a_mm"], 1)

            def norms(i, j):
                need(pe, sem["sq"], i * 8 + j + 1)
                pe.matmul(bank(0), same_head[:, :], sq[:, 0:UNIT], start=True, stop=True)
                pe.matmul(bank(1), same_head[:, :], sq[:, UNIT:], start=True, stop=True).then_inc(sem["n_mm"], 1)

            def scores(i, j):
                gather(sem["qk"], i * 8 + j + 1)
                gather(sem["masked"], i * 8 + j)
                if isinstance(i, int) and i + j == 0:
                    pe.wait_ge(n1.out, n1.n + NCH)
                    pe.sem_inc(sem["seen"], 1)
                t = qk[j % 2]
                for h in range(2):
                    for w in range(UNIT // WIN):
                        keys = (view(t, KOFF + WIN * w, [-WIN, 2], [1, WIN], p0=64 * h, rows=64) if w % 2 == 0
                                else view(t, KOFF + WIN * (w - 1), [1, 2 * WIN], p0=64 * h, rows=64))
                        mm = pe.matmul(view(ps, (4 + h) * CH + (w // 4) * 64, [1, 64], p0=WIN * (w % 4), rows=WIN),
                                       t[64 * h:64 * h + 64, WIN * w:WIN * w + WIN], keys, start=True, stop=True)
                mm.then_inc(sem["s_mm"], 1)

            def turn(i, j):
                need(pe, sem["p"], i * 8 + j + 1)
                need(pe, sem["ptz"], i * 8 + j)
                for t in range(4):
                    mm = pe.transpose(view(ps, 6 * CH + 128 * t, [1, 128]), s[j % 2][:, 128 * t:128 * t + 128], ident[:, :])
                mm.then_inc(sem["t_mm"], 1)

            def mix(i, j):
                gather(sem["ptz"], i * 8 + j + 1)
                gather(sem["o"], i * 8 + j)
                if j % 4 == 0:
                    gather(sem["v"], i * 8 + j + 4)
                for p in range(8):
                    n = 96 if p < 7 else 64
                    for h in range(2):
                        mm = pe.matmul(view(ps, 7 * CH + 64 * p, [1, n], p0=64 * h, rows=64),
                                       v[64 * h:64 * h + 64, p * CH + 64 * j:p * CH + 64 * j + 64],
                                       ptz[64 * h:64 * h + 64, 96 * p:96 * p + n],
                                       start=(p == 0), stop=(p == 7), skip_group_check=True)
                mm.then_inc(sem["pv_mm"], 1)

            def wo_part(i, lo, hi):
                need(pe, sem["o"], i * 8 + hi)
                if lo == 0:
                    need(pe, sem["wo"], (i // NU) * 16 + 16)
                    need(pe, sem["y2"], i + Y0)
                for j in range(lo, hi):
                    mm = pe.matmul(bank(3), wo[:, 128 * j:128 * j + 128], o[:, UNIT * j:UNIT * j + UNIT],
                                   start=(j == 0), stop=(j == NP - 1))
                if hi == NP:
                    mm.then_inc(sem["wo_mm"], 1)

            def mean(i):
                need(pe, sem["xs2"], i + 1)
                pe.matmul(bank(3), con.ones[:, :], xs2[:, :], start=True, stop=True).then_inc(sem["mean"], 1)

            def variance(i, run):
                need(pe, sem["sq2"], i + 1)
                if run:
                    need(pe, sem["v"], i * 8 + 8 + 7)
                pe.matmul(bank(2), con.ones[:, :], sq2[:, :], start=True, stop=True).then_inc(sem["var"], 1)

            def gate_mm(i, f):
                if f == 0:
                    need(pe, sem["xn"], i + 1)
                    need(pe, sem["w1"], (i // NU) * 16 + 16)
                f0, n = FB[f]
                pe.matmul(view(ps, GBANK[f] * CH, [1, CH], rows=n), w1[:, DI + f0:DI + f0 + n], xn[:, :],
                          start=True, stop=True).then_inc(sem["g_mm"], 1)

            def hid_mm(i, f):
                if f:
                    need(pe, sem["hid"], i * 3 + f + H0_)
                f0, n = FB[f]
                pe.matmul(view(ps, 3 * CH, [1, CH], rows=n), w1[:, f0:f0 + n], xn[:, :],
                          start=True, stop=True).then_inc(sem["h_mm"], 1)

            def w2_mm(i):
                need(pe, sem["w2"], (i // NU) * 16 + 16)
                need(pe, sem["hid"], i * 3 + 3 + H0_)
                for f, (f0, n) in enumerate(FB):
                    mm = pe.matmul(bank(3), w2[0:n, f * C:f * C + C], hid[0:n, f * UNIT:f * UNIT + UNIT],
                                   start=(f == 0), stop=(f == 2))
                mm.then_inc(sem["w2_mm"], 1)

            def slot(i, j, run, more, before):
                k = i - 1
                has, u, a = (run, i, j + 2) if j < 6 else (more, i + 1, j - 6)
                had1, u1, b1 = (run, i, j - 1) if j >= 1 else (before, k, 7)
                had2, u2, b2 = (run, i, j - 2) if j >= 2 else (before, k, j + 6)
                if run:
                    scores(i, j)
                if before and j == 2:
                    wo_part(k, 6, 8)
                if before and j == 6:
                    need(pe, sem["ln"], i * 8 + 8 if run else 0)
                    gate_mm(k, 1)
                    gate_mm(k, 2)
                if j == 6 and had2:
                    mix(u2, b2)
                if has:
                    if j == 7:
                        values(u, a)
                    project(u, a)
                    if j != 7:
                        values(u, a)
                if j != 6 and had2:
                    mix(u2, b2)
                if before and j < 2:
                    wo_part(k, 3 * j, 3 * j + 3)
                if before and j == 3:
                    mean(k)
                if before and j == 6:
                    hid_mm(k, 1)
                if before and j == 7:
                    hid_mm(k, 2)
                if had1:
                    turn(u1, b1)
                if has:
                    norms(u, a)
                if before and j == 4:
                    variance(k, run)
                if before and j == 5:
                    if run:
                        need(pe, sem["v"], i * 8 + 8)
                    gate_mm(k, 0)
                    hid_mm(k, 0)
                if before and j == 7:
                    w2_mm(k)

            n1.tensor(pe, con.ones, n1_banks, x)
            pe.wait_ge(sem["const"], n_const)
            pe.wait_ge(sem["zero"], 1)

            def behind(j):
                if j == 6:
                    n2.var_mm(pe, con.ones, n2_bank[0], 0)
                if j == 7:
                    n2.var_mm(pe, con.ones, n2_bank[1], 1)
                for c in {2: range(3), 7: range(3, 4)}.get(j, ()):
                    pe.wait_ge(sem["y2"], ended(c))
                    n2.mean_mm(pe, con.ones, n2_bank[c], y, c)
                if j == 7:
                    n2.var_mm(pe, con.ones, n2_bank[2], 2)
                    n2.var_mm(pe, con.ones, n2_bank[3], 3)

            iterations(pe, slot, behind)

        @block.scalar
        def _(act):
            def value_copy(i, q):
                need(act, sem["v_mm"], i * 8 + q + 1)
                if q % 4 == 0:
                    need(act, sem["pv_mm"], i * 8 - 4 + q)
                for r in range(2):
                    for h in range(2):
                        ins = act.activation(view(v, (2 * (q % 4) + r) * CH + 256 * (q // 4), [64, 4], [1, 64], p0=64 * h, rows=64),
                                             view(ps, 2 * CH + 64 * h, [128, 4], [1, 64], p0=64 * r, rows=64), ACT.Copy)
                ins.then_inc(sem["v"], 1)

            def raw_copy(i, j):
                need(act, sem["a_mm"], i * 8 + j + 1)
                need(act, sem["shuf"], i * 8 + j)
                need(act, sem["straight"], i * 8 + j)
                act.activation(view(raw, 0, [UNIT, 2], [1, UNIT]), bank(0, 2), ACT.Copy).then_inc(sem["raw"], 1)
                need(act, sem["raw"], i * 8 + j + 1)
                need(act, sem["n_mm"], i * 8 + j)
                act.activation(sq[:, :], raw[:, :], ACT.Square).then_inc(sem["sq"], 1)

            def inverse_norm(i, j):
                need(act, sem["n_mm"], i * 8 + j + 1)
                need(act, sem["qk"], i * 8 + j)
                act.activation(view(rn, 0, [UNIT, 2], [1, UNIT]), bank(0, 2), ACT.Ln, scale=float(2.0 ** 20)).then_inc(sem["ln"], 1)
                need(act, sem["ln"], i * 8 + j + 1)
                act.activation(rn[:, :], rn[:, :], ACT.Exp, scale=-0.5, bias=con.lift).then_inc(sem["rn"], 1)

            def spread(i, j):
                need(act, sem["t_mm"], i * 8 + j + 1)
                need(act, sem["pv_mm"], i * 8 + j)
                act.activation(view(ptz, 32, [96, 8], [1, 32]), view(ps, 6 * CH + 32, [64, 8], [1, 32]), ACT.Copy)
                act.activation(view(ptz, 0, [96, 8], [1, 32]), view(ps, 6 * CH, [64, 8], [1, 32]), ACT.Copy,
                               scale=halves[:, 0:1])
                act.activation(view(ptz, 64, [96, 7], [1, 32]), view(ps, 6 * CH + 64, [64, 7], [1, 32]), ACT.Copy,
                               scale=halves[:, 1:2]).then_inc(sem["ptz"], 1)

            def out_copy(i, j):
                need(act, sem["pv_mm"], i * 8 + j + 1)
                if j == 0:
                    need(act, sem["wo_mm"], i)
                act.activation(o[:, UNIT * j:UNIT * j + UNIT], bank(7), ACT.Copy).then_inc(sem["o"], 1)

            def gelu(i, f):
                n = FB[f][1]
                need(act, sem["g_mm"], i * 3 + f + 1)
                act.activation(gate[0:n, f * UNIT:f * UNIT + UNIT], view(ps, GBANK[f] * CH, [1, CH], rows=n),
                               ACT.Gelu, bias=fcol[0:n, 5 + f:6 + f]).then_inc(sem["gelu"], 1)

            def slot(i, j, run, more, before):
                k = i - 1
                has, u, a = (run, i, j + 2) if j < 6 else (more, i + 1, j - 6)
                had1, u1, b1 = (run, i, j - 1) if j >= 1 else (before, k, 7)
                had2, u2, b2 = (run, i, j - 2) if j >= 2 else (before, k, j + 6)
                if j == 0:
                    nc.scalar.preload_act_table_set(ACT_SET)
                if before and j == 6:
                    gelu(k, 1)
                    gelu(k, 2)
                    nc.scalar.preload_act_table_set(ACT_SET)
                if has:
                    raw_copy(u, a)
                if before and j == 4:
                    need(act, sem["cen"], k + 1)
                    act.activation(sq2[:, :], cen[:, :], ACT.Square).then_inc(sem["sq2"], 1)
                if has and j == 5:
                    value_copy(u, a)
                if run:
                    need(act, sem["shift"], i * 8 + j + 1)
                    act.activation(s[j % 2][:, :], s[j % 2][:, :], ACT.Exp, scale=8.0).then_inc(sem["exp"], 1)
                if has and j != 5:
                    value_copy(u, a)
                if before and j == 5:
                    need(act, sem["scaled"], k + 1)
                    act.activation(xn[:, :], xn[:, :], ACT.Identity, scale=fcol[:, 0:1], bias=fcol[:, 1:2]).then_inc(sem["xn"], 1)
                if had2:
                    out_copy(u2, b2)
                if had1:
                    spread(u1, b1)
                if has:
                    inverse_norm(u, a)
                if before and j == 4:
                    need(act, sem["var"], k + 1)
                    act.activation(sq2[:, :], bank(2), ACT.Ln, bias=con.eps).then_inc(sem["ln2"], 1)
                    need(act, sem["ln2"], k + 1)
                    act.activation(sq2[:, :], sq2[:, :], ACT.Exp, scale=-0.5).then_inc(sem["rs2"], 1)
                if before and j == 5:
                    gelu(k, 0)

            nc.scalar.preload_act_table_set(ACT_SET)
            n1.scalar(act, n1_banks, con.eps)
            act.wait_ge(sem["const"], n_const)

            def behind(j):
                if j == 5:
                    for c in range(3):
                        n2.square(act, c)
                if j == 6:
                    n2.root(act, n2_bank[0], con.eps, 0)
                if j == 7:
                    n2.root(act, n2_bank[1], con.eps, 1)
                    n2.square(act, 3)
                    n2.root(act, n2_bank[2], con.eps, 2)
                    n2.root(act, n2_bank[3], con.eps, 3)

            iterations(act, slot, behind)

        @block.gpsimd
        def _(pool):
            def straight(i, j):
                need(pool, sem["raw"], i * 8 + j + 1)
                need(pool, sem["tab"], i + 1)
                need(pool, sem["qk"], i * 8 + j)
                pool.tensor_tensor(view(rot, 0, [S, 4], [1, S]), view(raw, 0, [S, 4], [1, S]),
                                   view(tab_c, 0, [S, 2], [0, 2], [1, S]), ALU.mult).then_inc(sem["straight"], 1)
                need(pool, sem["straight"], i * 8 + j + 1)
                need(pool, sem["turned"], i * 8 + j + 1)
                pool.tensor_tensor(rot[:, :], rot[:, :], shuf[:, :], ALU.add).then_inc(sem["rot"], 1)

            def slot(i, j, run, more, before):
                has, u, a = (run, i, j + 2) if j < 6 else (more, i + 1, j - 6)
                if has:
                    straight(u, a)

            iterations(pool, slot, lambda j: None)

        @block.vector
        def _(dve):
            def shift_in(to, unit, done):
                dve.tensor_scalar(to[0:64, :], y[0:64, bass.ds(unit * UNIT, UNIT)], 1.0, None, ALU.mult)
                for b in range(2):
                    mm = dve.tensor_scalar(to[64:128, b * S + 1:b * S + S], y[64:128, bass.ds(unit * UNIT + b * S, S - 1)],
                                           1.0, None, ALU.mult)
                mm.then_inc(done, 1)

            def tables(i):
                need(dve, sem["straight"], i * 8)
                need(dve, sem["turned"], i * 8)
                for k in range(2):
                    for tab, base, n in ((tab_c, base_c, 0), (tab_s, base_s, 1)):
                        ins = dve.tensor_scalar(tab[:, k * S:k * S + S], base[:, k * S:k * S + S],
                                                cols[:, bass.ds((i // NU) * 13 + (2 * k + n), 1)], None, ALU.mult)
                ins.then_inc(sem["tab"], 1)

            def rotate(i, j):
                need(dve, sem["raw"], i * 8 + j + 1)
                need(dve, sem["rot"], i * 8 + j)
                dve.sem_inc(sem["ahead"], 1)
                dve.stream_shuffle(shuf[:, :], raw[:, :], [(p + 16) % 32 for p in range(32)]).then_inc(sem["shuf"], 1)
                need(dve, sem["shuf"], i * 8 + j + 1)
                need(dve, sem["tab"], i + 1)
                dve.tensor_tensor(view(shuf, 0, [S, 4], [1, S]), view(shuf, 0, [S, 4], [1, S]),
                                  view(tab_s, 0, [S, 2], [0, 2], [1, S]), ALU.mult).then_inc(sem["turned"], 1)

            def normalise(i, j):
                need(dve, sem["rot"], i * 8 + j + 1)
                need(dve, sem["rn"], i * 8 + j + 1)
                dve.scalar_tensor_tensor(out=view(qk[j % 2], 0, [KOFF, 2], [1, UNIT]), in0=view(rn, 0, [UNIT, 2], [1, UNIT]),
                                         scalar=1e12, in1=view(rot, 0, [UNIT, 2], [1, UNIT]),
                                         op0=ALU.min, op1=ALU.mult).then_inc(sem["qk"], 1)

            def soft_a(i, j):
                t = s[j % 2]
                need(dve, sem["s_mm"], i * 8 + j + 1)
                need(dve, sem["t_mm"], i * 8 + j - 1)
                dve.tensor_tensor(view(t, 0, [64, 2], [128, 4], [1, 64]), view(ps, 4 * CH, [CH, 2], [64, 4], [1, 64]),
                                  view(mask, 0, [0, 2], [64, 4], [1, 64]), ALU.add).then_inc(sem["masked"], 1)
                need(dve, sem["masked"], i * 8 + j + 1)
                dve.tensor_reduce(mx[:, :], view(t, 0, [64, 8], [1, 64]), AX.X, ALU.max).then_inc(sem["max"], 1)
                need(dve, sem["max"], i * 8 + j + 1)
                dve.tensor_tensor(view(t, 0, [64, 8], [1, 64]), view(t, 0, [64, 8], [1, 64]), view(mx, 0, [1, 8], [0, 64]),
                                  ALU.subtract).then_inc(sem["shift"], 1)

            def soft_b(i, j):
                t = s[j % 2]
                need(dve, sem["exp"], i * 8 + j + 1)
                dve.tensor_reduce(sm[:, :], view(t, 0, [64, 8], [1, 64]), AX.X, ALU.add).then_inc(sem["sum"], 1)
                need(dve, sem["sum"], i * 8 + j + 1)
                dve.reciprocal(rc[:, :], sm[:, :]).then_inc(sem["rcp"], 1)
                need(dve, sem["rcp"], i * 8 + j + 1)
                dve.tensor_tensor(view(t, 0, [64, 8], [1, 64]), view(t, 0, [64, 8], [1, 64]), view(rc, 0, [1, 8], [0, 64]),
                                  ALU.mult).then_inc(sem["p"], 1)

            def hidden(i, f):
                n = FB[f][1]
                need(dve, sem["h_mm"], i * 3 + f + 1)
                need(dve, sem["gelu"], i * 3 + f + 1 + G0)
                dve.scalar_tensor_tensor(out=hid[0:n, f * UNIT:f * UNIT + UNIT], in0=view(ps, 3 * CH, [1, CH], rows=n),
                                         scalar=fcol[0:n, 2 + f:3 + f], in1=gate[0:n, f * UNIT:f * UNIT + UNIT],
                                         op0=ALU.add, op1=ALU.mult).then_inc(sem["hid"], 1)

            def slot(i, j, run, more, before):
                k = i - 1
                has, u, a = (run, i, j + 2) if j < 6 else (more, i + 1, j - 6)
                next1, u1, a1 = (run, i, j + 1) if j < 7 else (more, i + 1, 0)
                ycol = y[:, bass.ds((k % NU) * UNIT, UNIT)] if before else None
                if run:
                    soft_a(i, j)
                if before and j == 6:
                    hidden(k, 0)
                if before and j == 7:
                    hidden(k, 2)
                if next1:
                    normalise(u1, a1)
                if j == 6 and more:
                    tables(i + 1)
                if has:
                    rotate(u, a)
                if before and j == 6:
                    hidden(k, 1)
                if run:
                    soft_b(i, j)
                if before and j == 2:
                    need(dve, sem["wo_mm"], k + 1)
                    dve.tensor_tensor(ycol, ycol, bank(3), ALU.add).then_inc(sem["y1"], 1)
                    need(dve, sem["y1"], k + 1)
                    shift_in(xs2, k % NU, sem["xs2"])
                if before and j == 3:
                    need(dve, sem["gelu"], k * 3 + G0)
                    dve.tensor_scalar(fcol[:, :], cols[:, bass.ds((k // NU) * 13 + 4, 9)], 1.0, None, ALU.mult).then_inc(sem["fcol"], 1)
                    need(dve, sem["mean"], k + 1)
                    need(dve, sem["xs2"], k + 1)
                    dve.tensor_tensor(cen[:, :], xs2[:, :], bank(3), ALU.subtract).then_inc(sem["cen"], 1)
                if before and j == 4:
                    need(dve, sem["rs2"], k + 1)
                    need(dve, sem["fcol"], k + 1)
                    dve.tensor_tensor(xn[:, :], cen[:, :], sq2[:, :], ALU.mult).then_inc(sem["scaled"], 1)
                if before and j == 7:
                    need(dve, sem["w2_mm"], k + 1)
                    dve.scalar_tensor_tensor(out=ycol, in0=bank(3), scalar=fcol[:, 8:9], in1=ycol,
                                             op0=ALU.add, op1=ALU.add).then_inc(sem["y2"], 1)
                if j == 5 and more:
                    need(dve, sem["a_mm"], (i + 1) * 8)
                    need(dve, sem["v_mm"], (i + 1) * 8)
                    need(dve, sem["y2"], i + 2 - NU + Y0)
                    shift_in(xs, (i + 1) % NU, sem["xs"])

            dve.sem_inc(sem["y2"], Y0)
            dve.sem_inc(sem["hid"], H0_)
            dve.sem_inc(sem["gelu"], G0)
            for t in (xs, xs2):
                dve.memset(view(t, 0, [S, 2], [1, 1], p0=64, rows=64), 0.0)
            for t in qk:
                mm = dve.memset(t[:, UNIT:KOFF], 0.0)
            mm.then_inc(sem["zero"], 1)
            n1.vector_centre(dve, n1_banks, x)
            n1.vector_scale(dve, y)
            dve.wait_ge(n1.out, n1.n + NCH)
            dve.wait_ge(sem["zero"], 1)
            dve.wait_ge(sem["const"], n_const)

            def behind(j):
                for c in {3: range(3), 7: range(3, 4)}.get(j, ()):
                    n2.centre(dve, n2_bank[c], y, c)
                for c in range(NCH if j == 7 else 0):
                    n2.scale(dve, n2_out, c)
                    n2.add(dve, n2_out, x, added, c)

            iterations(dve, slot, behind)

        body.close()


def state_space(nc, io, x, con):
    BF16 = mybir.dt.bfloat16
    K = DN // 128
    with Pool(nc) as m:
        ps = m.mem.enter_context(nc.psum_tensor("s_ps", [128, 8 * CH], F32))
        wl, wr = m.sb("s_wl", DN), m.sb("s_wr", DN)
        wd, wbc, wo = m.sb("s_wd", K * DN), m.sb("s_wbc", K * 2 * DS), m.sb("s_wo", K * C)
        cols = m.sb("s_cols", K * 8)
        alog, aneg, ae, al = (m.sb(f"s_{n}", DS) for n in ("alog", "aneg", "ae", "al"))
        ones2 = m.sb("s_ones2", C)
        z = m.sb("s_z", T)
        left, xl, gate, delta, dx = (m.sb(f"s_{n}", K * T) for n in ("left", "xl", "gate", "delta", "dx"))
        bc, res = m.sb("s_bc", T, rows=32), m.sb("s_res", T, rows=32)
        parts = m.mem.enter_context(nc.sbuf_tensor("s_parts", [96, T], BF16))
        bc_part = m.mem.enter_context(nc.sbuf_tensor("s_bcpart", [32, T], BF16))
        pick = m.mem.enter_context(nc.sbuf_tensor("s_pick", [96, 2 * DS * C], BF16))
        decay, st, prod = ([[m.sb(f"s_{n}{par}{k}", T // 2) for k in range(K)] for par in range(2)]
                           for n in ("decay", "state", "prod"))
        bs, cs = ([m.sb(f"s_{n}{par}", T // 2) for par in range(2)] for n in ("bs", "cs"))
        ident = m.sb("s_ident", C)
        ysum, squares = left, xl
        bank = lambda k, n=1, rows=128: view(ps, k * CH, [1, n * CH], rows=rows)

        sem = {n: m.sem("s_" + n) for n in (
            "load pick left_mm left conv xl right_mm gate dpre_mm dpre dabs dexp dlog bc_mm bc split "
            "a_in a0 a1 a2 zero dx fin b_mm c_mm b_in c_in decay drive scan prod acc seen gated mean cen sq var lv rstd nrm aff o_mm o").split()}
        loads = [(wl[:, :], io["s_wl"]), (wr[:, :], io["s_wr"]), (cols[:, :], io["s_cols"]), (wd[:, :], io["s_wd"]),
                 (wbc[:, :], io["s_wbc"]), (wo[:, :], io["s_wo"]), (alog[:, :], io["s_alog"]),
                 (ones2[:, :], io["k_ones2"]), (ident[:, :], io["k_ident"]), (dx[0:96, :], io["k_pick"])]
        n_load = 16 * len(loads)
        n1 = Norm(m, con, "s_ln1", (xl, xl[:, T:2 * T]))
        n1_banks = [bank(k) for k in range(8)]
        last = Norm(m, con, "s_ln2", (dx[:, 0:T], dx[:, T:2 * T]))
        added = m.sem("s_added")
        D0, D1 = 2 * K, 2
        body = ExitStack()
        block = body.enter_context(nc.Block())
        part = lambda k, c: slice(k * T + c * CH, k * T + c * CH + CH)
        H = T // 2

        @block.sync
        def _(sp):
            load(sp, sem["load"], loads)

        @block.tensor
        def _(pe):
            n1.tensor(pe, con.ones, n1_banks, x)
            pe.wait_ge(sem["load"], n_load)
            for c in range(NCH):
                pe.wait_ge(n1.out, n1.n + (c + 1 if c else 2))
                for k in range(K):
                    if c >= 2:
                        pe.wait_ge(sem["left"], 2 * (c - 2) + k + 1)
                    pe.matmul(bank(2 * (c % 2) + k), wl[:, 128 * k:128 * k + 128], z[:, c * CH:c * CH + CH],
                              start=True, stop=True).then_inc(sem["left_mm"], 1)
                for k in range(K):
                    if c:
                        pe.wait_ge(sem["gate"], 2 * (c - 1) + k + 1)
                    pe.matmul(bank(4 + k), wr[:, 128 * k:128 * k + 128], z[:, c * CH:c * CH + CH],
                              start=True, stop=True).then_inc(sem["right_mm"], 1)
            for c in range(NCH):
                pe.wait_ge(sem["xl"], 2 * c + 2)
                for k in range(K):
                    if c >= 2:
                        pe.wait_ge(sem["dpre"], 2 * (c - 2) + k + 1)
                    else:
                        pe.wait_ge(sem["left"], 2 * (c + 2) + k + 1)
                    for r in range(K):
                        mm = pe.matmul(bank(2 * (c % 2) + k), wd[:, r * DN + 128 * k:r * DN + 128 * k + 128],
                                       xl[:, part(r, c)], start=(r == 0), stop=(r == K - 1))
                    mm.then_inc(sem["dpre_mm"], 1)
                if c >= 2:
                    pe.wait_ge(sem["bc"], c - 1)
                for r in range(K):
                    mm = pe.matmul(bank(6 + c % 2, rows=32), wbc[:, 32 * r:32 * r + 32], xl[:, part(r, c)],
                                   start=(r == 0), stop=(r == K - 1))
                mm.then_inc(sem["bc_mm"], 1)
            pe.wait_ge(sem["pick"], 1)
            pe.wait_ge(sem["dpre"], 2 * NCH)
            pe.wait_ge(sem["bc"], NCH)
            pe.wait_ge(sem["gate"], 2 * NCH)

            def spread(h, n):
                g = h * DS + n
                for half, used, done in ((0, "b_in", "b_mm"), (1, "c_in", "c_mm")):
                    pe.wait_ge(sem[used], g + D1)
                    for c in range(2):
                        mm = pe.matmul(bank(4 + 2 * half + c), pick[:, bass.ds((n + half * DS) * C, C)],
                                       parts[:, h * H + c * CH:h * H + c * CH + CH], start=True, stop=True)
                    mm.then_inc(sem[done], 1)

            def add(h, n, par, first=False):
                g = h * DS + n
                for k in range(K):
                    pe.wait_ge(sem["prod"], g * K + k + 1 + D0)
                    for c in range(2):
                        mm = pe.matmul(bank(2 * k + c), ident[:, :], prod[par][k][:, c * CH:c * CH + CH],
                                       start=first, stop=True, skip_group_check=True)
                    mm.then_inc(sem["acc"], 1)

            def mean(c):
                for k in range(K):
                    mm = pe.matmul(bank(4 + c), ones2[:, :], ysum[:, part(k, c)], start=(k == 0), stop=(k == K - 1))
                mm.then_inc(sem["mean"], 1)

            for h in range(2):
                pe.wait_ge(sem["split"], 12 * (h + 1))
                for n in range(4):
                    spread(h, n)
                    if n == 2 and h:
                        pe.wait_ge(sem["gated"], K)
                    if n >= 2:
                        add(h, n - 2, n % 2, first=(n == 2))
                with pe.Fori(2, DS // 2) as n2:
                    for par in range(2):
                        spread(h, n2 * 2 + par)
                        add(h, n2 * 2 + (par - 2), par)
                if h:
                    pe.wait_ge(sem["b_in"], 2 * DS + D1)
                    mean(0)
                    mean(1)
                add(h, DS - 2, 0)
                add(h, DS - 1, 1)
            pe.wait_ge(sem["c_in"], 2 * DS + D1)
            pe.wait_ge(sem["gated"], 2 * K)
            mean(2)
            mean(3)
            for c in range(NCH):
                pe.wait_ge(sem["sq"], K * (c + 1))
                for k in range(K):
                    mm = pe.matmul(bank(c), ones2[:, :], squares[:, part(k, c)], start=(k == 0), stop=(k == K - 1))
                mm.then_inc(sem["var"], 1)
            for c in range(NCH):
                pe.wait_ge(sem["aff"], K * (c + 1))
                for k in range(K):
                    mm = pe.matmul(bank(4 + c), wo[:, C * k:C * k + C], ysum[:, part(k, c)], start=(k == 0), stop=(k == K - 1))
                mm.then_inc(sem["o_mm"], 1)
            for c in range(NCH):
                pe.wait_ge(sem["o"], c + 1)
                last.mean_mm(pe, con.ones, bank(c), z, c)
            for c in range(NCH):
                last.var_mm(pe, con.ones, bank(4 + c), c)

        @block.scalar
        def _(act):
            def silu_xl(c):
                for k in range(K):
                    act.wait_ge(sem["conv"], 8 * c + 4 * k + 4)
                    act.activation(xl[:, part(k, c)], delta[:, part(k, c)], ACT.Silu).then_inc(sem["xl"], 1)

            def delta_in(c):
                for k in range(K):
                    act.wait_ge(sem["dpre_mm"], 2 * c + k + 1)
                    act.activation(delta[:, part(k, c)], bank(2 * (c % 2) + k), ACT.Identity,
                                   bias=cols[:, 8 * k + 5:8 * k + 6]).then_inc(sem["dpre"], 1)
                act.wait_ge(sem["bc_mm"], c + 1)
                act.activation(bc[:, c * CH:c * CH + CH], bank(6 + c % 2, rows=32), ACT.Copy).then_inc(sem["bc"], 1)
                for k in range(K):
                    act.wait_ge(sem["dpre"], 2 * c + k + 1)
                    act.activation(left[:, part(k, c)], delta[:, part(k, c)], ACT.Abs).then_inc(sem["dabs"], 1)

            nc.scalar.preload_act_table_set(ACT_SET)
            n1.scalar(act, n1_banks, con.eps)
            act.wait_ge(sem["load"], n_load)
            for c in range(NCH):
                for k in range(K):
                    act.wait_ge(sem["left_mm"], 2 * c + k + 1)
                    act.activation(left[:, part(k, c)], bank(2 * (c % 2) + k), ACT.Copy).then_inc(sem["left"], 1)
                for k in range(K):
                    act.wait_ge(sem["right_mm"], 2 * c + k + 1)
                    act.activation(gate[:, part(k, c)], bank(4 + k), ACT.Silu).then_inc(sem["gate"], 1)
            for c in range(NCH):
                silu_xl(c)
                if c in (1, 2):
                    delta_in(c - 1)
            nc.scalar.preload_act_table_set(ACT_SET)
            act.activation(ae[:, :], alog[:, :], ACT.Abs).then_inc(sem["a0"], 1)
            act.wait_ge(sem["a0"], 1)
            act.activation(ae[:, :], ae[:, :], ACT.Exp, scale=-1.0).then_inc(sem["a1"], 1)
            act.wait_ge(sem["a1"], 1)
            act.activation(al[:, :], ae[:, :], ACT.Ln, bias=1.0).then_inc(sem["a2"], 1)

            def soft(h):
                for k in range(K):
                    a = slice(k * T + h * H, k * T + h * H + H)
                    act.wait_ge(sem["dabs"], 2 * K * (h + 1))
                    act.activation(left[:, a], left[:, a], ACT.Exp, scale=-1.0).then_inc(sem["dexp"], 1)
                    act.wait_ge(sem["dexp"], h * K + k + 1)
                    act.activation(left[:, a], left[:, a], ACT.Ln, bias=1.0).then_inc(sem["dlog"], 1)
            soft(0)
            delta_in(2)
            delta_in(3)
            act.wait_ge(sem["a_in"], 3)
            act.wait_ge(sem["zero"], 1)
            nc.scalar.preload_act_table_set(ACT_SET)

            def copy(of, mm, used, to, done, g):
                act.wait_ge(sem[mm], g + 1)
                act.wait_ge(sem[used], g * K - K + D0)
                act.activation(view(to, 0, [1, H]), view(ps, of * CH, [1, H]), ACT.Copy).then_inc(sem[done], 1)

            def step(h, n, par):
                g = h * DS + n
                copy(4, "b_mm", "drive", bs[par], "b_in", g)
                for k in range(K):
                    act.wait_ge(sem["scan"], g * K + k - 2 * K + 1 + D0)
                    act.sem_inc(sem["seen"], 1)
                    act.activation(view(decay[par][k], 1, [S, B // 2], [1, S - 1]),
                                   view(delta, k * T + h * H + 1, [S, B // 2], [1, S - 1]),
                                   ACT.Exp, scale=aneg[:, bass.ds(n, 1)]).then_inc(sem["decay"], 1)
                copy(6, "c_mm", "prod", cs[par], "c_in", g)

            for h in range(2):
                if h:
                    soft(h)
                act.wait_ge(sem["fin"], K * (h + 1))
                with act.Fori(0, DS // 2) as n2:
                    step(h, n2 * 2, 0)
                    step(h, n2 * 2 + 1, 1)
            for c in range(NCH):
                for k in range(K):
                    act.wait_ge(sem["cen"], K * c + k + 1)
                    act.activation(squares[:, part(k, c)], ysum[:, part(k, c)], ACT.Square).then_inc(sem["sq"], 1)

            def affine(c):
                for k in range(K):
                    act.wait_ge(sem["nrm"], K * c + k + 1)
                    act.activation(ysum[:, part(k, c)], ysum[:, part(k, c)], ACT.Identity, scale=cols[:, 8 * k + 6:8 * k + 7],
                                   bias=cols[:, 8 * k + 7:8 * k + 8]).then_inc(sem["aff"], 1)

            for c in range(NCH):
                a = slice(c * CH, c * CH + CH)
                act.wait_ge(sem["var"], c + 1)
                act.activation(z[:, a], bank(c), ACT.Ln, bias=con.eps).then_inc(sem["lv"], 1)
                act.wait_ge(sem["lv"], c + 1)
                act.activation(z[:, a], z[:, a], ACT.Exp, scale=-0.5).then_inc(sem["rstd"], 1)
                if c:
                    affine(c - 1)
            affine(NCH - 1)
            for c in range(NCH):
                act.wait_ge(sem["o_mm"], c + 1)
                act.activation(z[:, c * CH:c * CH + CH], bank(4 + c), ACT.Copy).then_inc(sem["o"], 1)
            last.scalar(act, n1_banks, con.eps)

        @block.gpsimd
        def _(pool):
            for par in range(2):
                for k in range(K):
                    zero = pool.memset(view(decay[par][k], 0, [S, B // 2], [1, 1]), 0.0)
            zero.then_inc(sem["zero"], 1)
            pool.wait_ge(sem["load"], n_load)
            pool.tensor_copy(pick[:, :], dx[0:96, :]).then_inc(sem["pick"], 1)

            def step(h, n, par):
                g = h * DS + n
                for k in range(K):
                    pool.wait_ge(sem["scan"], g * K + k + 1 + D0)
                    pool.wait_ge(sem["c_in"], g + 1 + D1)
                    pool.wait_ge(sem["acc"], g * K + k - 2 * K + 1 + D0)
                    pool.tensor_tensor(prod[par][k][:, :], st[par][k][:, :], cs[par][:, :], ALU.mult).then_inc(sem["prod"], 1)

            for h in range(2):
                with pool.Fori(0, DS // 2) as n2:
                    step(h, n2 * 2, 0)
                    step(h, n2 * 2 + 1, 1)

        @block.vector
        def _(dve):
            for n in ("scan", "drive", "prod", "acc"):
                dve.sem_inc(sem[n], D0)
            for n in ("b_in", "c_in"):
                dve.sem_inc(sem[n], D1)
            n1.vector_centre(dve, n1_banks, x)
            n1.vector_scale(dve, z)
            dve.wait_ge(sem["load"], n_load)
            for c in range(NCH):
                for k in range(K):
                    tap = lambda t: cols[:, 8 * k + t:8 * k + t + 1]
                    at, n = k * T + c * CH, 8 * c + 4 * k
                    dve.wait_ge(sem["left"], 2 * c + k + 1)
                    dve.tensor_scalar(delta[:, part(k, c)], left[:, part(k, c)], tap(3), tap(4), ALU.mult,
                                      ALU.add).then_inc(sem["conv"], 1)
                    for s in range(1, 4):
                        dve.wait_ge(sem["conv"], n + s)
                        dve.scalar_tensor_tensor(out=view(delta, at + s, [S, 2], [1, S - s]),
                                                 in0=view(left, at, [S, 2], [1, S - s]), scalar=tap(3 - s),
                                                 in1=view(delta, at + s, [S, 2], [1, S - s]),
                                                 op0=ALU.mult, op1=ALU.add).then_inc(sem["conv"], 1)
            def split(c):
                a, n = slice(c * CH, c * CH + CH), 6 * c
                dve.wait_ge(sem["bc"], c + 1)
                dve.tensor_copy(parts[0:32, a], bc[:, a]).then_inc(sem["split"], 1)
                dve.wait_ge(sem["split"], n + 1)
                dve.tensor_tensor(res[:, a], bc[:, a], parts[0:32, a], ALU.subtract).then_inc(sem["split"], 1)
                dve.wait_ge(sem["split"], n + 2)
                dve.tensor_copy(bc_part[:, a], res[:, a]).then_inc(sem["split"], 1)
                dve.wait_ge(sem["split"], n + 3)
                dve.tensor_tensor(bc[:, a], res[:, a], bc_part[:, a], ALU.subtract).then_inc(sem["split"], 1)
                dve.tensor_copy(parts[32:64, a], bc_part[:, a]).then_inc(sem["split"], 1)
                dve.wait_ge(sem["split"], n + 4)
                dve.tensor_copy(parts[64:96, a], bc[:, a]).then_inc(sem["split"], 1)

            split(0)
            split(1)
            dve.wait_ge(sem["a2"], 1)
            dve.tensor_scalar(aneg[:, :], alog[:, :], 0.0, None, ALU.max).then_inc(sem["a_in"], 1)
            dve.wait_ge(sem["a_in"], 1)
            dve.tensor_tensor(aneg[:, :], aneg[:, :], al[:, :], ALU.add).then_inc(sem["a_in"], 1)
            dve.wait_ge(sem["a_in"], 2)
            dve.tensor_scalar(aneg[:, :], aneg[:, :], -1.0, None, ALU.mult).then_inc(sem["a_in"], 1)
            dve.wait_ge(sem["pick"], 1)

            def drives(h):
                for k in range(K):
                    a, n = slice(k * T + h * H, k * T + h * H + H), h * K + k
                    dve.wait_ge(sem["dlog"], n + 1)
                    dve.scalar_tensor_tensor(out=delta[:, a], in0=delta[:, a], scalar=0.0, in1=left[:, a],
                                             op0=ALU.max, op1=ALU.add).then_inc(sem["dx"], 1)
                    dve.wait_ge(sem["dx"], 3 * n + 1)
                    dve.tensor_scalar(delta[:, a], delta[:, a], 1e-4, 10.0, ALU.max, ALU.min).then_inc(sem["dx"], 1)
                    dve.wait_ge(sem["dx"], 3 * n + 2)
                    dve.sem_inc(sem["fin"], 1)
                    dve.tensor_tensor(dx[:, a], delta[:, a], xl[:, a], ALU.mult).then_inc(sem["dx"], 1)
                dve.wait_ge(sem["dx"], 3 * K * (h + 1))
            drives(0)
            split(2)

            def step(h, n, par):
                g = h * DS + n
                for k in range(K):
                    dve.wait_ge(sem["b_in"], g + 1 + D1)
                    dve.wait_ge(sem["prod"], g * K + k - 2 * K + 1 + D0)
                    dve.tensor_tensor(st[par][k][:, :], dx[:, k * T + h * H:k * T + h * H + H], bs[par][:, :],
                                      ALU.mult).then_inc(sem["drive"], 1)
                for k in range(K):
                    dve.wait_ge(sem["drive"], g * K + k + 1 + D0)
                    dve.wait_ge(sem["decay"], g * K + k + 1)
                    dve.tensor_tensor_scan(st[par][k][:, :], decay[par][k][:, :], st[par][k][:, :], 0.0, ALU.mult,
                                           ALU.add).then_inc(sem["scan"], 1)

            def centre(c):
                dve.wait_ge(sem["mean"], c + 1)
                for k in range(K):
                    dve.tensor_tensor(ysum[:, part(k, c)], ysum[:, part(k, c)], bank(4 + c), ALU.subtract).then_inc(sem["cen"], 1)

            for h in range(2):
                with dve.Fori(0, DS // 2) as n2:
                    step(h, n2 * 2, 0)
                    step(h, n2 * 2 + 1, 1)
                if h == 0:
                    split(3)
                    drives(1)
                else:
                    centre(0)
                    centre(1)
                for k in range(K):
                    a = slice(k * T + h * H, k * T + h * H + H)
                    dve.wait_ge(sem["acc"], (h + 1) * DS * K - K + k + 1 + D0)
                    dve.tensor_tensor(ysum[:, a], gate[:, a], view(ps, 2 * k * CH, [1, H]), ALU.mult).then_inc(sem["gated"], 1)
            centre(2)
            centre(3)
            for c in range(NCH):
                dve.wait_ge(sem["rstd"], c + 1)
                for k in range(K):
                    dve.wait_ge(sem["sq"], K * c + k + 1)
                    dve.tensor_tensor(ysum[:, part(k, c)], ysum[:, part(k, c)], z[:, c * CH:c * CH + CH], ALU.mult).then_inc(sem["nrm"], 1)
            last.vector_centre(dve, n1_banks, z)
            last.vector_scale(dve, gate[:, 0:T], x, added)

        body.close()


def experts(nc, io, x, con):
    BE, HB = B * E8, HID // 128
    with Pool(nc) as m:
        ps = m.mem.enter_context(nc.psum_tensor("e_ps", [128, 8 * CH], F32))
        gate, ident, iota = m.sb("e_gate", E8), m.sb("e_ident", C), m.sb("e_iota", CAP)
        z, zn = m.sb("e_z", T), m.sb("e_zn", T)
        pn, sn = m.sb("e_pn", 2 * BE), m.sb("e_sn", 2 * BE)
        mx, sm, rc = (m.sb(f"e_{n}", 16) for n in ("max", "sum", "rcp"))
        row, mark, slot = (m.sb(f"e_{n}", S, rows=BE) for n in ("row", "mark", "slot"))
        zero_row = m.sb("e_zero", S, rows=BE)
        top = m.sb("e_top", 8, rows=BE)
        hot, hotp = ([m.sb(f"e_{n}{b}", 2 * 1024) for b in range(2)] for n in ("hot", "hotp"))
        back = m.sb("e_back", 4 * B * S)
        xin = m.sb("e_xin", E8 * CH)
        w1, w2 = ([m.sb(f"e_{n}{b}", HID) for b in range(2)] for n in ("w1", "w2"))
        h = [m.sb(f"e_h{b}", HB * CH) for b in range(2)]
        yout = m.sb("e_y", 4 * 2 * CH)
        bank = lambda k, n=CH, col=0, rows=128: view(ps, k * CH + col, [1, n], rows=rows)
        load_s, w_s = m.sem("e_load"), [m.sem(f"e_weights{b}") for b in range(2)]
        names = ("score max sub exp sum rcp prob zn_mm zn row_mm row top strike mark count slot back_mm sn hot gather xin "
                 "weigh turn_mm back h_mm h y_mm y out_mm out").split()
        sem = {n: m.sem("e_" + n) for n in names}
        loads = [(gate[:, :], io["e_gate"]), (ident[:, :], io["k_ident"]), (iota[:, :], io["k_iota"])]

        def weights(sp, e, b):
            sp.dma_start(w1[b][:, :], io["e_w1"][e]).then_inc(w_s[b], 16)
            sp.dma_start(w2[b][:, :], io["e_w2"][e]).then_inc(w_s[b], 16)

        n1 = Norm(m, con, "e_ln1", (back, xin))
        n1_banks = [bank(k) for k in range(8)]
        n2, n2_banks = Norm(m, con, "e_ln2", (h[0], h[1])), n1_banks[4:] + n1_banks[:4]
        added = m.sem("e_added")
        body = ExitStack()
        block = body.enter_context(nc.Block())

        @block.sync
        def _(sp):
            load(sp, load_s, loads)
            for b in range(2):
                weights(sp, b, b)
            with sp.Fori(1, E8 // 2) as g:
                for b in range(2):
                    sp.wait_ge(sem["y_mm"], 2 * g + b + 1)
                    weights(sp, 2 * g + b, b)

        @block.tensor
        def _(pe):
            n1.tensor(pe, con.ones, n1_banks, x)
            pe.wait_ge(load_s, 16 * len(loads))
            pe.wait_ge(n1.out, n1.n + NCH)
            for half in range(2):
                for b in range(B):
                    mm = pe.matmul(bank(0, E8, half * BE + b * E8), z[:, (2 * b + half) * 128:(2 * b + half) * 128 + 128],
                                   gate[:, :], start=True, stop=True)
            mm.then_inc(sem["score"], 1)
            for t in range(16):
                mm = pe.transpose(bank(1 + t // 4, 128, 128 * (t % 4)), z[:, 128 * t:128 * t + 128], ident[:, :])
                if t % 4 == 3:
                    mm.then_inc(sem["zn_mm"], 1)
            pe.wait_ge(sem["prob"], 1)
            for half in range(2):
                mm = pe.transpose(bank(5, 128, 128 * half, rows=BE), pn[:, BE * half:BE * half + BE], ident[:, :])
            mm.then_inc(sem["row_mm"], 1)
            pe.wait_ge(sem["slot"], 2)
            for half in range(2):
                mm = pe.transpose(bank(6, BE, BE * half), slot[:, 128 * half:128 * half + 128], ident[0:BE, 0:BE])
            mm.then_inc(sem["back_mm"], 1)

            def gather(g):
                pe.wait_ge(sem["hot"], 2 * g + 2)
                for b in (2 * g, 2 * g + 1):
                    if b == 0:
                        pe.wait_ge(sem["zn"], 4)
                    if b >= 2:
                        pe.wait_ge(sem["xin"], b - 1)
                    for half in range(2):
                        t = 2 * b + half
                        at = half * 1024 + (b % 2) * CH
                        mm = pe.matmul(bank(b % 2), zn[:, 128 * t:128 * t + 128], hot[g % 2][:, at:at + CH],
                                       start=(half == 0), stop=(half == 1))
                    mm.then_inc(sem["gather"], 1)

            def turn(g):
                pe.wait_ge(sem["weigh"], 2 * g + 2)
                for q in range(4):
                    if g:
                        pe.wait_ge(sem["back"], 4 * (g - 1) + q + 1)
                    for p in range(2):
                        for half in range(2):
                            at = half * 1024 + (2 * q + p) * 128
                            mm = pe.transpose(bank(2 + q, 128, p * S + half * 128), hotp[g % 2][:, at:at + 128], ident[:, :])
                    mm.then_inc(sem["turn_mm"], 1)

            gather(0)
            for g in range(4):
                if g < 3:
                    gather(g + 1)
                turn(g)
            pe.wait_ge(sem["back"], 16)
            pe.wait_ge(sem["xin"], B)
            with pe.Fori(0, E8 // 2) as g:
                for b in range(2):
                    pe.wait_ge(w_s[b], (g + 1) * 32)
                    for k in range(HB):
                        pe.wait_ge(sem["h"], (g * 2 + b) * HB + k + 1)
                        pe.matmul(bank(k), w1[b][:, 128 * k:128 * k + 128], xin[:, bass.ds((g * 2 + b) * CH, CH)],
                                  start=True, stop=True).then_inc(sem["h_mm"], 1)
                    pe.wait_ge(sem["y"], g * 2 + b + 1)
                    for k in range(HB):
                        pe.wait_ge(sem["h"], (g * 2 + b + 1) * HB + k + 1)
                        for q in range(4):
                            mm = pe.matmul(bank(4 + b, 128, 128 * q), h[b][:, k * CH + 128 * q:k * CH + 128 * q + 128],
                                           w2[b][:, 128 * k:128 * k + 128], start=(k == 0 and q == 0), stop=(k == HB - 1),
                                           skip_group_check=True)
                    mm.then_inc(sem["y_mm"], 1)
            pe.wait_ge(sem["y"], E8 + 2)
            for b in range(B):
                for p in range(E8 // 2):
                    at = p * 1024 + (b % 2) * CH + (b // 2) * 128
                    mm = pe.matmul(bank(b // 2, S, (b % 2) * S), yout[:, at:at + 128],
                                   back[:, (b * 4 + p) * S:(b * 4 + p) * S + S], start=(p == 0), stop=(p == 3))
                if b % 2:
                    mm.then_inc(sem["out_mm"], 1)
            for c in range(NCH):
                pe.wait_ge(sem["out"], c + 1)
                n2.mean_mm(pe, con.ones, bank(4 + c), z, c)
            for c in range(NCH):
                n2.var_mm(pe, con.ones, bank(c), c)

        @block.scalar
        def _(act):
            nc.scalar.preload_act_table_set(ACT_SET)
            n1.scalar(act, n1_banks, con.eps)
            act.wait_ge(sem["sub"], 1)
            act.activation(pn[:, :], pn[:, :], ACT.Exp).then_inc(sem["exp"], 1)
            for n in range(4):
                act.wait_ge(sem["zn_mm"], n + 1)
                act.activation(zn[:, n * CH:n * CH + CH], bank(1 + n), ACT.Copy).then_inc(sem["zn"], 1)

            def back_copy(g):
                for q in range(4):
                    act.wait_ge(sem["turn_mm"], 4 * g + q + 1)
                    act.activation(back[:, (g * E8 + 2 * q) * S:(g * E8 + 2 * q + 2) * S], bank(2 + q),
                                   ACT.Copy).then_inc(sem["back"], 1)

            for g in range(4):
                for b in (2 * g, 2 * g + 1):
                    act.wait_ge(sem["gather"], b + 1)
                    act.activation(view(xin, b * CAP, [CH, E8], [1, CAP]), view(ps, (b % 2) * CH, [CAP, E8], [1, CAP]),
                                   ACT.Copy).then_inc(sem["xin"], 1)
                if g:
                    back_copy(g - 1)
            back_copy(3)
            with act.Fori(0, E8 // 2) as g:
                for b in range(2):
                    for k in range(HB):
                        act.wait_ge(sem["h_mm"], (g * 2 + b) * HB + k + 1)
                        act.wait_ge(sem["y_mm"], g * 2 + b + 1)
                        act.activation(h[b][:, k * CH:k * CH + CH], bank(k), ACT.Gelu).then_inc(sem["h"], 1)
            for n in range(4):
                act.wait_ge(sem["out_mm"], n + 1)
                act.activation(z[:, n * CH:n * CH + CH], bank(n), ACT.Copy).then_inc(sem["out"], 1)
            nc.scalar.preload_act_table_set(ACT_SET)
            n2.scalar(act, n2_banks, con.eps)

        @block.gpsimd
        def _(pool):
            for g in range(4):
                for half in range(2):
                    pool.wait_ge(sem["hot"], 2 * g + half + 1)
                    if g >= 2:
                        pool.wait_ge(sem["turn_mm"], 4 * (g - 1))
                    pool.tensor_tensor(view(hotp[g % 2], half * 1024, [CAP, 16], [1, CAP]),
                                       view(hot[g % 2], half * 1024, [CAP, 16], [1, CAP]),
                                       view(pn, half * BE + 2 * g * E8, [1, 16], [0, CAP]), ALU.mult).then_inc(sem["weigh"], 1)

        @block.vector
        def _(dve):
            dve.sem_inc(sem["h"], HB)
            dve.sem_inc(sem["y_mm"], 2)
            dve.sem_inc(sem["y"], 2)
            n1.vector_centre(dve, n1_banks, x)
            n1.vector_scale(dve, z)
            p3 = view(pn, 0, [E8, 16], [1, E8])
            dve.wait_ge(sem["score"], 1)
            dve.tensor_reduce(mx[:, :], view(ps, 0, [E8, 16], [1, E8]), AX.X, ALU.max).then_inc(sem["max"], 1)
            dve.wait_ge(sem["max"], 1)
            dve.tensor_tensor(p3, view(ps, 0, [E8, 16], [1, E8]), view(mx, 0, [1, 16], [0, E8]), ALU.subtract).then_inc(sem["sub"], 1)
            dve.wait_ge(sem["exp"], 1)
            dve.tensor_reduce(sm[:, :], p3, AX.X, ALU.add).then_inc(sem["sum"], 1)
            dve.wait_ge(sem["sum"], 1)
            dve.reciprocal(rc[:, :], sm[:, :]).then_inc(sem["rcp"], 1)
            dve.wait_ge(sem["rcp"], 1)
            dve.tensor_tensor(p3, p3, view(rc, 0, [1, 16], [0, E8]), ALU.mult).then_inc(sem["prob"], 1)
            dve.wait_ge(sem["row_mm"], 1)
            dve.memset(zero_row[:, :], 0.0)
            dve.tensor_copy(row[:, :], bank(5, S, rows=BE)).then_inc(sem["row"], 1)
            dve.wait_ge(sem["row"], 1)
            for r in range(CAP // 8):
                dve.max(top[:, :], row[:, :]).then_inc(sem["top"], 1)
                dve.wait_ge(sem["top"], r + 1)
                dve.match_replace(row[:, :], top[:, :], row[:, :], -1.0).then_inc(sem["strike"], 1)
                dve.wait_ge(sem["strike"], r + 1)
            dve.tensor_scalar(mark[:, :], row[:, :], 0.0, None, ALU.is_lt).then_inc(sem["mark"], 1)
            dve.wait_ge(sem["mark"], 1)
            dve.tensor_tensor_scan(slot[:, :], mark[:, :], zero_row[:, :], 0.0, ALU.add, ALU.add).then_inc(sem["count"], 1)
            dve.wait_ge(sem["count"], 1)
            dve.tensor_tensor(slot[:, :], slot[:, :], mark[:, :], ALU.mult).then_inc(sem["slot"], 1)
            dve.wait_ge(sem["slot"], 1)
            dve.tensor_scalar(slot[:, :], slot[:, :], -1.0, None, ALU.add).then_inc(sem["slot"], 1)
            dve.wait_ge(sem["back_mm"], 1)
            dve.tensor_copy(sn[:, :], bank(6, 2 * BE)).then_inc(sem["sn"], 1)
            dve.wait_ge(sem["sn"], 1)
            dve.wait_ge(load_s, 16 * len(loads))
            for g in range(4):
                for half in range(2):
                    if g >= 2:
                        dve.wait_ge(sem["gather"], 2 * (g - 1))
                        dve.wait_ge(sem["weigh"], 2 * (g - 1))
                    dve.tensor_tensor(view(hot[g % 2], half * 1024, [CAP, 16], [1, CAP]),
                                      view(sn, half * BE + 2 * g * E8, [1, 16], [0, CAP]),
                                      view(iota, 0, [0, 16], [1, CAP]), ALU.is_equal).then_inc(sem["hot"], 1)
            with dve.Fori(0, E8 // 2) as g:
                for b in range(2):
                    dve.wait_ge(sem["y_mm"], g * 2 + b + 3)
                    for r in range(2):
                        ins = dve.tensor_scalar(yout[64 * b:64 * b + 64, bass.ds(g * 1024 + r * CH, CH)],
                                                view(ps, (4 + b) * CH, [1, CH], p0=64 * r, rows=64), 1.0, None, ALU.mult)
                    ins.then_inc(sem["y"], 1)
            n2.vector_centre(dve, n2_banks, z)
            n2.vector_scale(dve, zn, x, added)

        body.close()


class Constants:

    def __init__(self, nc, ctx, io):
        self.norm_sems = [ctx.enter_context(nc.semaphore(f"norm_{x}")) for x in
                          ("mean", "centred", "squared", "var", "logvar", "rstd", "normed")]
        self.norms_before = 0

        def sb(name, cols, rows=128):
            return ctx.enter_context(nc.sbuf_tensor(name, [rows, cols], F32))

        self.ones = sb("k_ones", C)
        self.head8 = sb("k_head8", C, rows=H0)
        self.eps_t = sb("k_eps", 1)
        self.eps = self.eps_t[:, 0:1]
        self.lift_t = sb("k_lift", 1)
        self.lift = self.lift_t[:, 0:1]
        self.loads = [(self.lift_t[:, :], io["k_lift"]), (self.ones[:, :], io["k_ones"]), (self.head8[:, :], io["k_head8"]), (self.eps_t[:, :], io["k_eps"])]


def sandwich(nc, io, out):
    with ExitStack() as sems, ExitStack() as ctx:
        x = ctx.enter_context(nc.sbuf_tensor("x_t", [128, T], F32))
        con = Constants(nc, ctx, io)
        landed = sems.enter_context(nc.semaphore("landed"))
        with nc.Block() as block:
            @block.sync
            def _(sp):
                pairs = [(x[:, c * CH:(c + 1) * CH], io["x"][:, c * CH:(c + 1) * CH]) for c in range(NCH)]
                sp.wait_ge(landed, load(sp, landed, pairs + con.loads))
        additive_attention(nc, io, x, con)
        local_attention(nc, io, x, con)
        state_space(nc, io, x, con)
        experts(nc, io, x, con)
        store = sems.enter_context(nc.semaphore("store"))
        with nc.Block() as block:
            @block.sync
            def _(sp):
                for c in range(NCH):
                    sp.dma_start(out[:, c * CH:(c + 1) * CH], x[:, c * CH:(c + 1) * CH]).then_inc(store, 16)
                sp.wait_ge(store, 16 * NCH)


def dim_order():
    q, r = np.divmod(np.arange(DH), 32)
    order = np.where(r < 16, 16 * q + r, 32 + 16 * q + r - 16)
    return order, (order + 32) % 64


def constants():

    f = np.float32
    k = {"k_ones": np.full((C, C), 1.0 / C, f)}
    k["k_head8"] = np.repeat(np.eye(H0, dtype=f), DH0, axis=1)
    k["k_lift"] = np.full((C, 1), 10 * np.log(2.0), f)
    k["k_ident"] = np.eye(C, dtype=f)
    k["k_same"] = np.kron(np.eye(2, dtype=f), np.ones((DH, DH), f))
    half = np.arange(0, DH, 2, dtype=f)
    freqs = np.arange(S, dtype=f)[:, None] * (f(1.0) / f(10000.0) ** (half / f(DH)))[None, :]
    freqs = np.concatenate([freqs, freqs], -1)
    base = (half + f(0.4 * DH)) / f(1.4 * DH)
    power = (np.arange(S, dtype=f) - f(S // 2)) / f(WIN // 2)
    xscale = base[None, :] ** power[:, None]
    xscale = np.concatenate([xscale, xscale], -1).astype(f)
    order, _ = dim_order()
    sign = np.where(np.arange(DH) < DH // 2, f(-1), f(1))
    for name, t in (("k_cos", np.cos(freqs)), ("k_sin", np.sin(freqs) * sign)):
        qk = np.concatenate([(t * xscale).T[order], (t * (f(1.0) / xscale)).T[order]], 1)
        k[name] = np.ascontiguousarray(np.tile(qk, (2, 1)).astype(f))
    i, c = np.arange(128)[:, None] % WIN, np.arange(2 * WIN)[None, :]
    even = (np.arange(128)[:, None] // WIN) % 2 == 0
    own = (c < WIN) == even
    seen = np.where(own, c % WIN <= i, c % WIN >= i)
    first = seen & (own | (np.arange(128)[:, None] >= WIN))
    k["k_mask"] = np.concatenate([np.where(z, f(0), f(NEG)) for z in (first, seen, first, seen)], 1)
    k["k_ones2"] = np.full((C, C), 1.0 / DN, f)
    pick = np.tile(np.eye(2 * DS, dtype=f)[:, :, None], (3, 1, C)).reshape(6 * DS, 2 * DS * C)
    k["k_pick"] = pick
    k["k_iota"] = np.tile(np.arange(CAP, dtype=f), (C, 1))
    lower = (np.arange(128) % 64 < WIN).astype(f)
    k["k_halves"] = np.stack([lower, 1 - lower], 1)
    k["k_eps"] = np.full((C, 1), LN_EPS, f)
    return k


def arrange(i):
    def col(a):
        return np.ascontiguousarray(np.asarray(a).reshape(-1, 1))

    a = {"x": np.ascontiguousarray(np.asarray(i["L0_attn_hidden_states"]).reshape(T, C).T)}
    for n in ("Wq", "Wk", "Wt", "Wqa", "Wka"):
        a["a_" + n.lower()] = np.ascontiguousarray(i["L0_attn_" + n])
    for n in ("bq", "bk", "bt", "bqa", "bka"):
        a["a_" + n] = col(i["L0_attn_" + n])
    order, partner = dim_order()
    wqkv = np.asarray(i["L0_ffn_Wqkv"]).reshape(DEPTH, C, 3, HEADS, DH)
    a["f_wq"], a["f_wk"] = (np.ascontiguousarray(wqkv[:, :, n][..., order].reshape(DEPTH, C, INNER)) for n in range(2))
    a["f_wv"] = np.ascontiguousarray(wqkv[:, :, 2].reshape(DEPTH, C, INNER))
    a["f_wo"] = np.ascontiguousarray(np.asarray(i["L0_ffn_Wo"]).reshape(DEPTH, NP, 128, C).transpose(0, 2, 1, 3).reshape(DEPTH, 128, INNER))
    a["f_w1"] = np.ascontiguousarray(i["L0_ffn_W1"])
    w2 = np.zeros((DEPTH, 3, 128, C), np.float32)
    b1 = np.zeros((DEPTH, 2, 3, 128), np.float32)
    b1_in = np.asarray(i["L0_ffn_b1"]).reshape(DEPTH, 2, DI)
    for f, (f0, n) in enumerate(FB):
        w2[:, f, :n] = np.asarray(i["L0_ffn_W2"])[:, f0:f0 + n]
        b1[:, :, f, :n] = b1_in[:, :, f0:f0 + n]
    a["f_w2"] = np.ascontiguousarray(w2.transpose(0, 2, 1, 3).reshape(DEPTH, 128, 3 * C))
    cols = np.zeros((128, DEPTH, 13), np.float32)
    for n, name in enumerate(("q_scale", "k_scale")):
        g = np.asarray(i["L0_ffn_" + name]).T
        for t, o in enumerate((order, partner)):
            cols[:, :, 2 * n + t] = np.concatenate([g[o], g[o]], 0)
    cols[:, :, 4], cols[:, :, 5], cols[:, :, 12] = (np.asarray(i["L0_ffn_" + n]).T for n in ("ln_g", "ln_b", "b2"))
    cols[:, :, 6:12] = b1.transpose(3, 0, 1, 2).reshape(128, DEPTH, 6)
    a["f_cols"] = cols.reshape(128, DEPTH * 13)

    def rows(w):
        w = np.asarray(w)
        return np.ascontiguousarray(w.reshape(-1, 128, w.shape[1]).transpose(1, 0, 2).reshape(128, -1))

    L3 = {n[8:]: np.asarray(v) for n, v in i.items() if n.startswith("L1_attn_")}
    a["s_wl"], a["s_wr"] = np.ascontiguousarray(L3["W_left"].T), np.ascontiguousarray(L3["W_right"].T)
    a["s_wd"], a["s_wo"] = rows(L3["W_delta"].T), rows(L3["W_out"].T)
    a["s_wbc"] = rows(np.concatenate([L3["W_B"], L3["W_C"]], 0).T)
    a["s_alog"] = np.ascontiguousarray(np.broadcast_to(L3["A_log"][None, :], (128, DS)))
    a["e_gate"], a["e_w1"] = (np.ascontiguousarray(i["L1_ffn_" + n]) for n in ("gate_w", "w1"))
    a["e_w2"] = np.ascontiguousarray(np.asarray(i["L1_ffn_w2"]).reshape(E8, HID // 128, 128, C).transpose(0, 2, 1, 3).reshape(E8, 128, HID))
    a["s_cols"] = rows(np.concatenate([L3["conv_w"].reshape(DN, 4)] + [L3[n].reshape(DN, 1) for n in
                                      ("conv_b", "b_delta", "ln_g", "ln_b")], 1))
    return a


def kernel(**inputs):
    import concourse.bacc as bacc
    from concourse.bass_utils import run_bass_kernel_spmd

    nc = bacc.Bacc("TRN2", target_bir_lowering=False, num_devices=1)
    arrays = {**arrange(inputs), **constants()}
    io = {n: nc.dram_tensor("in_" + n, a.shape, mybir.dt.from_np(a.dtype), kind="ExternalInput").ap() for n, a in arrays.items()}
    out = nc.dram_tensor("out_x", (C, T), F32, kind="ExternalOutput").ap()
    sandwich(nc, io, out)
    r = run_bass_kernel_spmd(nc, [{"in_" + n: a for n, a in arrays.items()}], core_ids=[0])
    return np.ascontiguousarray(r.results[0]["out_x"].T).reshape(B, S, C)
```
